# Optimizing a Trainium2 kernel written in Bass

```python
import numpy as np
import jax
import jax.numpy as jnp

def _softmax(x, axis=-1):
    return jax.nn.softmax(x, axis=axis)

def _gelu(x):
    return jax.nn.gelu(x, approximate=True)

def _silu(x):
    return jax.nn.silu(x)

def _sigmoid(x):
    return jax.nn.sigmoid(x)

def _layernorm(x, axis=-1, eps=1e-05):
    m = jnp.mean(x, axis=axis, keepdims=True)
    v = jnp.var(x, axis=axis, keepdims=True)
    return (x - m) / jnp.sqrt(v + eps)

def _scatter_add(tgt, idx, src, axis=0):
    return tgt.at[idx].add(src)

def _segment_sum(src, seg, n):
    return jax.ops.segment_sum(src, seg, n)
kernel_name = 'mk_adaln_ffn_d1_seqx_r2_87f809'

def setup_inputs(seed: int=0):
    np.random.seed(seed)
    _w = jnp.asarray

    def _rec_inputs():
        import jax
        import jax.numpy as jnp
        _rk = jax.random.key(seed)
        x = -0.000125 + 0.9999 * jax.random.normal(jax.random.fold_in(_rk, 1), (32, 128, 2048), jnp.float32)
        _lenS = 128 - jax.random.randint(jax.random.fold_in(_rk, 7), (32,), 0, max(1, 128 // 4) + 1, jnp.int32)
        _lenS2 = 128 - jax.random.randint(jax.random.fold_in(_rk, 8), (32,), 0, max(1, 128 // 4) + 1, jnp.int32)
        cond_128 = 0.0061147 + 1.02565 * jax.random.normal(jax.random.fold_in(_rk, 11), (32, 128), jnp.float32)
        fside_S_0 = -0.022604 + 0.987366 * jax.random.normal(jax.random.fold_in(_rk, 12), (128,), jnp.float32)
        return (x, cond_128, fside_S_0)
    x, cond_128, fside_S_0 = _rec_inputs()

    def _L0_cond_setup():
        import jax, jax.numpy as jnp
        import numpy as np
        from jax import lax
        N, C_IN, L = (32, 128, 2048)
        C_OUT, K, GROUPS = (128, 9, 4)
        C_DIM, PAD, STRIDE = (128, 4, 1)
        key = jax.random.key(seed)
        k1, k2, k3, k4, k5 = jax.random.split(key, 5)
        x = jax.random.normal(k1, (N, C_IN, L), dtype=jnp.float32)
        c = jax.random.normal(k2, (N, C_DIM), dtype=jnp.float32)
        weight = jax.random.normal(k3, (C_OUT, C_IN // GROUPS, K), dtype=jnp.float32)
        c_weight = jax.random.normal(k4, (C_OUT, C_DIM), dtype=jnp.float32)
        bias = jax.random.normal(k5, (C_OUT,), dtype=jnp.float32)
        return {'x': x, 'c': c, 'weight': weight, 'c_weight': c_weight, 'bias': bias}
    _L0_cond_all = _L0_cond_setup()
    _L0_cond_in = {k: v for k, v in _L0_cond_all.items() if k in ('weight', 'c_weight')}
    del _L0_cond_all

    def _L0_ffn_setup():
        import jax, jax.numpy as jnp
        import numpy as np
        SCALING = 16.0 / 8.0
        GAMMA = 1.0
        EPS = 1e-12
        key = jax.random.key(seed)
        ks = jax.random.split(key, 8)
        B, T, H, O = (4, 1024, 2048, 2048)
        E_tot, E_act, r = (16, 4, 8)
        return {'x': jax.random.normal(ks[0], (B, T, H), jnp.float32), 'W_base': jax.random.normal(ks[1], (O, H), jnp.float32) * 0.02, 'b_base': jax.random.normal(ks[2], (O,), jnp.float32) * 0.02, 'lora_A': jax.random.normal(ks[3], (E_tot, r, H), jnp.float32) * 0.02, 'lora_B': jax.random.normal(ks[4], (E_tot, O, r), jnp.float32) * 0.02, 'router_W': jax.random.normal(ks[5], (E_tot, H), jnp.float32) * 0.02, 'router_b': jax.random.normal(ks[6], (E_tot,), jnp.float32) * 0.02, 'domain_prior': jax.random.uniform(ks[7], (E_tot,), jnp.float32), 'active': jnp.arange(E_act, dtype=jnp.int32)}
    _L0_ffn_all = _L0_ffn_setup()
    _L0_ffn_in = {k: v for k, v in _L0_ffn_all.items() if k in ('W_base', 'b_base', 'lora_A', 'lora_B', 'router_W', 'router_b', 'domain_prior', 'active')}
    del _L0_ffn_all
    return {'x': x, 'cond_128': cond_128, 'fside_S_0': fside_S_0, 'L0_cond_weight': _L0_cond_in['weight'], 'L0_cond_c_weight': _L0_cond_in['c_weight'], 'L0_ffn_W_base': _L0_ffn_in['W_base'], 'L0_ffn_b_base': _L0_ffn_in['b_base'], 'L0_ffn_lora_A': _L0_ffn_in['lora_A'], 'L0_ffn_lora_B': _L0_ffn_in['lora_B'], 'L0_ffn_router_W': _L0_ffn_in['router_W'], 'L0_ffn_router_b': _L0_ffn_in['router_b'], 'L0_ffn_domain_prior': _L0_ffn_in['domain_prior'], 'L0_ffn_active': _L0_ffn_in['active']}

def reference(x, cond_128, fside_S_0, L0_cond_weight, L0_cond_c_weight, L0_ffn_W_base, L0_ffn_b_base, L0_ffn_lora_A, L0_ffn_lora_B, L0_ffn_router_W, L0_ffn_router_b, L0_ffn_domain_prior, L0_ffn_active):
    import jax
    import jax.numpy as jnp

    def _L0_cond_ref(x, c, weight, c_weight, bias):
        import jax, jax.numpy as jnp
        import numpy as np
        from jax import lax
        N, C_IN, L = (32, 128, 2048)
        C_OUT, K, GROUPS = (128, 9, 4)
        C_DIM, PAD, STRIDE = (128, 4, 1)
        out = lax.conv_general_dilated(x, weight, window_strides=(STRIDE,), padding=[(PAD, PAD)], dimension_numbers=('NCH', 'OIH', 'NCH'), feature_group_count=GROUPS)
        ctx = jnp.einsum('nd,od->no', c, c_weight)
        out = out + ctx[:, :, None] + bias[None, :, None]
        return out

    def _L0_ffn_ref(x, W_base, b_base, lora_A, lora_B, router_W, router_b, domain_prior, active):
        import jax, jax.numpy as jnp
        import numpy as np
        SCALING = 16.0 / 8.0
        GAMMA = 1.0
        EPS = 1e-12
        y = jnp.einsum('bth,oh->bto', x, W_base) + b_base
        A = lora_A[active]
        Bm = lora_B[active]
        z = jnp.einsum('bth,erh->bter', x, A)
        contribs = jnp.einsum('bter,eor->bteo', z, Bm) * SCALING
        logits = jnp.einsum('bth,eh->bte', x, router_W) + router_b
        logits = logits[..., active]
        prior = domain_prior[active]
        alpha = jax.nn.softmax(jnp.log(prior + EPS) + logits / GAMMA, axis=-1)
        return y + jnp.einsum('bteo,bte->bto', contribs, alpha)
    x = x + _L0_ffn_ref(_L0_cond_ref(x, cond_128, L0_cond_weight, L0_cond_c_weight, fside_S_0), L0_ffn_W_base, L0_ffn_b_base, L0_ffn_lora_A, L0_ffn_lora_B, L0_ffn_router_W, L0_ffn_router_b, L0_ffn_domain_prior, L0_ffn_active)
    return x

_drawn_inputs = setup_inputs


def setup_inputs(seed=0):
    import zlib

    import numpy as np

    out = dict(_drawn_inputs(seed))
    spreads = {}
    factors = {'L0_ffn_b_base': 52.647, 'L0_ffn_router_b': 200.0, 'L0_ffn_domain_prior': 200.0}
    for name, (base, spread) in spreads.items():
        noise = np.random.default_rng([zlib.crc32(name.encode()), seed]).standard_normal(out[name].shape)
        drawn = base * np.exp(spread * noise) if base else spread * noise
        out[name] = jnp.asarray(drawn.astype(out[name].dtype))
    for name, factor in factors.items():
        out[name] = (out[name] * factor).astype(out[name].dtype)
    return out
```

```python
from contextlib import ExitStack

import concourse.bass as bass
from concourse import mybir

ALU = mybir.AluOpType
ACT = mybir.ActivationFunctionType
AX = mybir.AxisListType
F32 = mybir.dt.float32
F16 = mybir.dt.float16
I32 = mybir.dt.int32
ABSMAX = bass.bass_isa.ReduceOp.absmax

P = 128
N = 32
L = 2048
O = 2048
G = 4
CG = 32
K = 9
R = 4
M = L // R
TAP = K + R - 1
OC = 512
NOC = O // OC
KB = L // P
MB = M // P
E = 16
EA = 4
RK = 8
ZR = EA * RK
ZC = ZR + EA
SCALING = 16.0 / 8.0
EPS = 1e-12
EXPONENT = 0x7F800000
TOP = 2.0 ** 13
UNTOP = 2.0 ** -14
FLOOR = 2.0 ** -40
LAG = 3
WAIT_BANKS = 2


def adaln_ffn(nc, xc, xr, wconv, condT, cwT, bias, wt, loraA, routerW, loraB, b_base, router_b, prior, active, out):
    ctx_rows = nc.dram_tensor("ctx_rows", (N, P), F32).ap()

    with ExitStack() as ctx:
        def sb(name, shape, dt):
            return ctx.enter_context(nc.sbuf_tensor(name, shape, dt))

        def sem(name):
            return ctx.enter_context(nc.semaphore(name))

        W16 = sb("W16", [P, (NOC * KB + LAG) * 2 * OC], F16)
        W32 = W16[:, :].bitcast(F32)
        xf = sb("xf", [P, G, M], F32)
        xh = sb("xh", [P, 2, G, M + 2], F16)
        hs = sb("hs", [P, 2, OC], F32)
        h16 = sb("h16", [P, 2, 2, KB, P], F16)
        T16 = sb("T16", [P, 2, G, (TAP) * CG], F16)
        A16 = sb("A16", [P, KB, 2 * ZC], F16)
        Bp = sb("Bp", [P, O], F32)
        xres = sb("xres", [P, 2, O], F32)
        ctxb = sb("ctxb", [P, P], F32)
        ctxs = sb("ctxs", [P, P], F32)
        ident = sb("ident", [P, P], F32)
        zcat = sb("zcat", [P, P], F32)
        zT = sb("zT", [P, P], F32)
        ones = zT[0:1, 0:P]
        biasr = zcat[0:1, 0:P]
        sc = sb("sc", [P, 2, 8], F32)
        tmp = sb("tmp", [P, 16], F32)
        yinv = sb("yinv", [P, 5], F32)
        cst = sb("cst", [P, 16], F32)
        cmx = sb("cmx", [P, 8], F32)
        wmx = sb("wmx", [P, NOC, 4], F32)
        wam = sb("wam", [P, NOC, 2], F32)
        wsc = sb("wsc", [P, NOC, 2], F32)
        amx = sb("amx", [P, 2], F32)
        zs = sb("zs", [P, 2 * ZC], F32)
        sm = sb("sm", [P, 24], F32)
        sel = sb("sel", [P, ZR], F32)
        selr = sb("selr", [P, EA], F32)
        acti = sb("acti", [P, EA], I32)
        part = sb("part", [P, 1], I32)
        actf = sb("actf", [P, 4, EA], F32)
        pcol = sb("pcol", [P, 1], F32)
        rbp = sb("rbp", [P, 4], F32)
        bias4 = sb("bias4", [P, EA], F32)

        A_raw = xres[:, 0, :]
        B_raw = xres[:, 1, :]
        R_raw = Bp[0:E, :]
        T32 = h16[:, 1, :, :, :].rearrange("p a k c -> p (a k c)").bitcast(F32)[:, 0:G * TAP * CG].rearrange("p (g c) -> p g c", g=G)
        AT32 = hs[:, :, :].rearrange("p a c -> p (a c)")[:, 0:KB * ZC].rearrange("p (k c) -> p k c", k=KB)
        cT_sb = xf[:, 0, 0:N]
        cwT_sb = xf[:, 1, 0:P]
        ctxn = xf[0:N, 2, 0:P]
        iot = xf[:, 3, 0:P]
        ioti = xf[:, 3, P:2 * P].bitcast(I32)
        rpbc = xf[0:E, 3, 2 * P:3 * P]

        Y = [ctx.enter_context(nc.psum_tensor(f"Y{i}", [P, OC], F32)) for i in range(NOC)]
        C = [ctx.enter_context(nc.psum_tensor(f"C{i}", [P, OC], F32)) for i in range(2)]
        Z = ctx.enter_context(nc.psum_tensor("Z", [P, OC], F32))
        Q = ctx.enter_context(nc.psum_tensor("Q", [P, OC], F32))

        in_act = sem("in_act")
        in_ctx = sem("in_ctx")
        in_T = sem("in_T")
        in_A = sem("in_A")
        in_B = sem("in_B")
        in_rb = sem("in_rb")
        in_b = sem("in_b")
        in_W = [sem(f"in_W{i}") for i in range(NOC)]
        pool_set = sem("pool_set")
        dve_set = sem("dve_set")
        dve_link = sem("dve_link")
        act_set = sem("act_set")
        pe_set = sem("pe_set")
        ctx_stored = sem("ctx_stored")
        w_max = sem("w_max")
        w_allmax = sem("w_allmax")
        w_scale = sem("w_scale")
        w_hi = sem("w_hi")
        w_lo = sem("w_lo")
        x_in = sem("x_in")
        xr_in = sem("xr_in")
        x_max = sem("x_max")
        x_allmax = sem("x_allmax")
        max_seen = sem("max_seen")
        x_scale = sem("x_scale")
        x_hi = sem("x_hi")
        x_lo = sem("x_lo")
        conv_done = sem("conv_done")
        bank_free = sem("bank_free")
        h_hi = sem("h_hi")
        h_lo = sem("h_lo")
        z_done = sem("z_done")
        dve_sm = sem("dve_sm")
        sm_step = sem("sm_step")
        scale_step = sem("scale_step")
        act_exp = sem("act_exp")
        z_ready = sem("z_ready")
        z_turned = sem("z_turned")
        zT_ready = sem("zT_ready")
        y_done = sem("y_done")
        y_free = sem("y_free")
        out_done = sem("out_done")

        block = ctx.enter_context(nc.Block())

        def wslot(oc, kb, half):
            at = ((oc * KB + kb) * 2 + half) * OC
            return W16[:, at:at + OC]

        def wraw(oc, kb, n=1):
            at = (oc * KB + kb + LAG) * OC
            return W32[:, at:at + n * OC]

        @block.sync
        def _(sp):
            def load_x(n):
                sp.dma_start(xf[:, :, :], xc[n]).then_inc(x_in, 16)
                sp.dma_start(ctxb[:, :], ctx_rows[n:n + 1, :].partition_broadcast(P) if isinstance(n, int) else
                             ctx_rows[bass.ds(n, 1), :].partition_broadcast(P)).then_inc(x_in, 16)

            def load_res(n, b):
                sp.dma_start(xres[:, b, :], xr[n]).then_inc(xr_in, 16)

            sp.dma_start(cT_sb, condT).then_inc(in_ctx, 16)
            sp.dma_start(cwT_sb, cwT).then_inc(in_ctx, 16)
            sp.dma_start(biasr, bias).then_inc(in_ctx, 16)
            sp.dma_start(acti[:, :], active.partition_broadcast(P)).then_inc(in_act, 16)
            sp.dma_start(rbp[0:E, 0:1], router_b).then_inc(in_rb, 16)
            sp.dma_start(rbp[0:E, 1:2], prior).then_inc(in_rb, 16)
            sp.wait_ge(dve_set, 1)
            for r in range(R):
                sp.dma_start(T32[r * CG:(r + 1) * CG, :, r * CG:(r + K) * CG], wconv).then_inc(in_T, 16)
            sp.dma_start(A_raw, loraA).then_inc(in_A, 16)
            sp.wait_ge(dve_set, 2)
            sp.dma_start(R_raw, routerW).then_inc(in_A, 16)
            sp.dma_start(B_raw, loraB).then_inc(in_B, 16)
            sp.dma_start(Bp[ZR:ZR + 1, :], b_base).then_inc(in_b, 16)
            sp.wait_ge(act_set, 1)
            sp.dma_start(ctx_rows, ctxn).then_inc(ctx_stored, 16)
            sp.wait_ge(ctx_stored, 16)
            sp.wait_ge(pe_set, 5)
            sp.wait_ge(dve_set, 8)
            load_x(0)
            for oc in range(NOC):
                for q in range(4):
                    sp.dma_start(wraw(oc, 4 * q, 4), wt[oc, :, q * 4 * OC:(q + 1) * 4 * OC]).then_inc(in_W[oc], 16)
                if oc == 0:
                    sp.wait_ge(x_hi, 1)
                    sp.wait_ge(x_lo, 1)
                    load_x(1)
                if oc == 1:
                    sp.wait_ge(pe_set, 5)
                    load_res(0, 0)
                    load_res(1, 1)
            sp.wait_ge(x_hi, 2)
            sp.wait_ge(x_lo, 2)
            load_x(2)

            def tile(t, b, more_x, more_res):
                def store(oc):
                    sp.wait_ge(y_free, 4 * t + oc + 1 + NOC)
                    sp.dma_start(out[t, :, oc * OC:(oc + 1) * OC], xres[:, b, oc * OC:(oc + 1) * OC]).then_inc(out_done, 16)

                store(0)
                store(1)
                if more_x:
                    sp.wait_ge(x_hi, t + 3)
                    sp.wait_ge(x_lo, t + 3)
                    load_x(t + 3)
                store(2)
                store(3)
                if more_res:
                    sp.wait_ge(out_done, 64 * (t + 1))
                    load_res(t + 2, b)

            with sp.Fori(0, N - 4, 2) as t:
                for b in range(2):
                    tile(t + b, b, True, True)
            tile(N - 4, 0, True, True)
            for t in range(N - 3, N):
                tile(t, t % 2, False, t < N - 2)
            sp.wait_ge(out_done, 64 * N)

        @block.gpsimd
        def _(pool):
            nc.gpsimd.iota(ioti, [[1, P]], base=0, channel_multiplier=0).then_inc(pool_set, 1)
            nc.gpsimd.iota(part[:, :], [[0, 1]], base=0, channel_multiplier=1).then_inc(pool_set, 1)
            nc.gpsimd.memset(xh[:, :, :, 0:1], 0.0).then_inc(pool_set, 1)
            nc.gpsimd.memset(xh[:, :, :, M + 1:M + 2], 0.0).then_inc(pool_set, 1)
            pool.wait_ge(dve_set, 8)
            nc.gpsimd.partition_all_reduce(cmx[:, 4:8], cmx[:, 0:4], P, ABSMAX).then_inc(pool_set, 1)
            for n in range(2):
                pool.wait_ge(x_max, n + 1)
                nc.gpsimd.partition_all_reduce(amx[:, 1:2], amx[:, 0:1], P, ABSMAX).then_inc(x_allmax, 1)
            for oc in range(NOC):
                pool.wait_ge(w_max, oc + 1)
                nc.gpsimd.partition_all_reduce(wam[:, oc, 1:2], wam[:, oc, 0:1], P, ABSMAX).then_inc(w_allmax, 1)

            def tile(t):
                pool.wait_ge(x_max, t + 3)
                pool.sem_inc(max_seen, 1)
                nc.gpsimd.partition_all_reduce(amx[:, 1:2], amx[:, 0:1], P, ABSMAX).then_inc(x_allmax, 1)

            with pool.Fori(0, N - 2, 1) as t:
                tile(t)

        @block.scalar
        def _(act):
            act.wait_ge(pe_set, 1)
            nc.scalar.copy(ctxn, Q[0:N, 0:P]).then_inc(act_set, 1)
            act.wait_ge(in_rb, 32)
            act.wait_ge(dve_set, 5)
            nc.scalar.activation(rbp[0:E, 2:3], rbp[0:E, 1:2], ACT.Ln).then_inc(act_set, 1)
            act.wait_ge(pe_set, 3)
            nc.scalar.copy(AT32[:, 0:KB // 2, :], C[0][:, 0:KB // 2 * ZC].rearrange("p (k c) -> p k c", c=ZC)).then_inc(act_set, 1)
            nc.scalar.copy(AT32[:, KB // 2:KB, :], C[1][:, 0:KB // 2 * ZC].rearrange("p (k c) -> p k c", c=ZC)).then_inc(act_set, 1)
            act.wait_ge(pe_set, 4)
            act.wait_ge(in_b, 16)
            for oc in range(NOC):
                nc.scalar.mul(Bp[0:ZR, oc * OC:(oc + 1) * OC], Y[oc][0:ZR, :], SCALING).then_inc(act_set, 1)
            act.wait_ge(dve_set, 9)
            nc.scalar.activation(A16[:, :, 0:ZR], AT32[:, :, 0:ZR], ACT.Copy, scale=cst[:, 2:3]).then_inc(act_set, 1)
            nc.scalar.activation(A16[:, :, ZR:ZC], AT32[:, :, ZR:ZC], ACT.Copy, scale=cst[:, 3:4]).then_inc(act_set, 1)
            nc.scalar.activation(T16[:, 0, :, :], T32, ACT.Copy, scale=cst[:, 0:1]).then_inc(act_set, 1)

            def split_x(n, b):
                act.wait_ge(x_scale, n + 1)
                nc.scalar.activation(xh[:, 0, :, 1:M + 1], xf[:, :, :], ACT.Copy, scale=sc[:, b, 1:2]).then_inc(x_hi, 1)

            def split_h(n, b, mb):
                act.wait_ge(bank_free, 4 * n + mb + 1 + WAIT_BANKS)
                nc.scalar.activation(h16[:, b, 0, 4 * mb:4 * mb + 4, :].rearrange("p k c -> p (k c)"), hs[:, mb % 2, :],
                                     ACT.Copy, scale=sc[:, b, 2:3]).then_inc(h_hi, 1)

            split_x(0, 0)
            for mb in range(MB):
                split_h(0, 0, mb)
            split_x(1, 1)
            for oc in range(NOC):
                act.wait_ge(w_scale, oc + 1)
                for kb in range(KB):
                    if oc * KB + kb >= LAG:
                        act.wait_ge(w_lo, oc * KB + kb - LAG + 1)
                    nc.scalar.activation(wslot(oc, kb, 0), wraw(oc, kb), ACT.Copy, scale=wsc[:, oc, 0:1]).then_inc(w_hi, 1)

            def tile(t, b, conv, split):
                act.wait_ge(dve_sm, 5 * t + 3)
                nc.scalar.activation(sm[:, 8:12], sm[:, 0:4], ACT.Exp, bias=sm[:, 4:5], accum_out=sm[:, 12:13]).then_inc(act_exp, 1)
                if conv:
                    split_h(t + 1, 1 - b, 0)
                    split_h(t + 1, 1 - b, 1)
                act.wait_ge(z_turned, t + 1)
                nc.scalar.copy(zT[:, :], Q[:, 0:P]).then_inc(zT_ready, 1)
                if conv:
                    split_h(t + 1, 1 - b, 2)
                    split_h(t + 1, 1 - b, 3)
                if split:
                    split_x(t + 2, b)

            with act.Fori(0, N - 2, 2) as t:
                for b in range(2):
                    tile(t + b, b, True, True)
            tile(N - 2, 0, True, False)
            tile(N - 1, 1, False, False)

        @block.vector
        def _(dve):
            nc.vector.memset(T32, 0.0).then_inc(dve_set, 1)
            nc.vector.memset(Bp[:, :], 0.0).then_inc(dve_set, 1)
            nc.vector.memset(ones, 1.0).then_inc(dve_set, 1)
            nc.vector.memset(cmx[:, 0:4], FLOOR).then_inc(y_free, NOC)
            nc.vector.memset(tmp[:, :], 0.0).then_inc(bank_free, WAIT_BANKS)
            dve.wait_ge(in_act, 16)
            step = [0]

            def link(ins):
                step[0] += 1
                ins.then_inc(dve_link, 1)
                dve.wait_ge(dve_link, step[0])

            link(nc.vector.tensor_copy(actf[:, 0, :], acti[:, :]))
            link(nc.vector.tensor_scalar(actf[:, 1, :], actf[:, 0, :], 0.0, float(E), ALU.is_lt, ALU.mult))
            link(nc.vector.tensor_tensor(actf[:, 2, :], actf[:, 0, :], actf[:, 1, :], ALU.add))
            link(nc.vector.tensor_scalar(actf[:, 3, :], actf[:, 2, :], 0.0, float(E - 1), ALU.max, ALU.min))
            dve.wait_ge(pool_set, 2)
            link(nc.vector.tensor_copy(iot, ioti))
            link(nc.vector.tensor_copy(pcol[:, :], part[:, :]))
            for j in range(EA):
                link(nc.vector.tensor_scalar(sm[:, j:j + 1], actf[:, 3, j:j + 1], float(RK), None, ALU.mult))
                link(nc.vector.tensor_scalar(sel[:, RK * j:RK * j + RK], iot[:, 0:RK], sm[:, j:j + 1], None, ALU.add))
            link(nc.vector.tensor_scalar(sel[:, :], sel[:, :], pcol[:, 0:1], None, ALU.is_equal))
            link(nc.vector.tensor_scalar(ident[:, :], iot, pcol[:, 0:1], None, ALU.is_equal))
            nc.vector.tensor_scalar(selr[:, :], actf[:, 3, :], pcol[:, 0:1], None, ALU.is_equal).then_inc(dve_set, 1)
            dve.wait_ge(in_rb, 32)
            nc.vector.tensor_scalar(rbp[0:E, 1:2], rbp[0:E, 1:2], EPS, None, ALU.add).then_inc(dve_set, 1)
            dve.wait_ge(act_set, 2)
            link(nc.vector.tensor_tensor(rbp[0:E, 3:4], rbp[0:E, 2:3], rbp[0:E, 0:1], ALU.add))
            link(nc.vector.memset(rpbc, 0.0))
            nc.vector.tensor_scalar(rpbc, rpbc, rbp[0:E, 3:4], None, ALU.add).then_inc(dve_set, 1)
            dve.wait_ge(pe_set, 5)
            nc.vector.tensor_copy(bias4[:, :], Z[:, 0:EA]).then_inc(dve_set, 1)
            dve.wait_ge(in_T, 64)
            link(nc.vector.tensor_reduce(cmx[:, 0:1], T32, AX.XY, ALU.max, apply_absolute_value=True))
            link(nc.vector.tensor_reduce(cmx[0:N, 1:2], ctxn, AX.X, ALU.max, apply_absolute_value=True))
            dve.wait_ge(act_set, 4)
            link(nc.vector.tensor_reduce(cmx[:, 2:3], AT32[:, :, 0:ZR], AX.XY, ALU.max, apply_absolute_value=True))
            link(nc.vector.tensor_reduce(cmx[:, 3:4], AT32[:, :, ZR:ZC], AX.XY, ALU.max, apply_absolute_value=True))
            nc.vector.memset(zcat[:, :], 0.0).then_inc(dve_set, 1)
            dve.wait_ge(pool_set, 5)
            link(nc.vector.tensor_scalar(cmx[:, 4:8], cmx[:, 4:8], FLOOR, None, ALU.max))
            link(nc.vector.tensor_scalar(cst[:, 0:4].bitcast(I32), cmx[:, 4:8].bitcast(I32), EXPONENT, EXPONENT, ALU.bitwise_and, ALU.bitwise_xor))
            link(nc.vector.tensor_scalar(cst[:, 4:8].bitcast(I32), cmx[:, 4:8].bitcast(I32), EXPONENT, None, ALU.bitwise_and))
            link(nc.vector.tensor_scalar(cst[:, 4:8], cst[:, 4:8], UNTOP, None, ALU.mult))
            link(nc.vector.tensor_scalar(cst[:, 8:9], cmx[:, 4:5], float(K * CG), None, ALU.mult))
            link(nc.vector.tensor_copy(cst[:, 9:10], cmx[:, 5:6]))
            nc.vector.tensor_scalar(cst[:, 0:4], cst[:, 0:4], TOP, None, ALU.mult).then_inc(dve_set, 1)
            dve.wait_ge(dve_set, 9)
            dve.wait_ge(act_set, 4 + NOC + 3)
            nc.vector.scalar_tensor_tensor(out=A16[:, :, ZC:ZC + ZR], in0=AT32[:, :, 0:ZR], scalar=cst[:, 2:3],
                                           in1=A16[:, :, 0:ZR], op0=ALU.mult, op1=ALU.subtract).then_inc(dve_set, 1)
            nc.vector.scalar_tensor_tensor(out=A16[:, :, ZC + ZR:2 * ZC], in0=AT32[:, :, ZR:ZC], scalar=cst[:, 3:4],
                                           in1=A16[:, :, ZR:ZC], op0=ALU.mult, op1=ALU.subtract).then_inc(dve_set, 1)
            nc.vector.scalar_tensor_tensor(out=T16[:, 1, :, :], in0=T32, scalar=cst[:, 0:1],
                                           in1=T16[:, 0, :, :], op0=ALU.mult, op1=ALU.subtract).then_inc(dve_set, 1)

            def max_x(n):
                dve.wait_ge(x_in, 32 * (n + 1))
                nc.vector.tensor_reduce(amx[:, 0:1], xf[:, :, :], AX.XY, ALU.max, apply_absolute_value=True).then_inc(x_max, 1)

            SCALE_STEPS = 7

            def scale_x(n, b):
                def wait(k):
                    dve.wait_ge(scale_step, SCALE_STEPS * n + k)

                if not (isinstance(n, int) and n == 0):
                    dve.wait_ge(h_lo, 4 * n)
                dve.wait_ge(x_allmax, n + 1)
                nc.vector.tensor_scalar(sc[:, b, 0:1], amx[:, 1:2], FLOOR, None, ALU.max).then_inc(scale_step, 1)
                wait(1)
                nc.vector.tensor_scalar(tmp[:, 0:1].bitcast(I32), sc[:, b, 0:1].bitcast(I32), EXPONENT, EXPONENT,
                                        ALU.bitwise_and, ALU.bitwise_xor)
                nc.vector.tensor_scalar(tmp[:, 1:2].bitcast(I32), sc[:, b, 0:1].bitcast(I32), EXPONENT, None, ALU.bitwise_and)
                nc.vector.tensor_scalar(tmp[:, 2:3], sc[:, b, 0:1], cst[:, 8:9], cst[:, 9:10], ALU.mult, ALU.add).then_inc(scale_step, 1)
                wait(2)
                nc.vector.tensor_scalar(tmp[:, 3:4].bitcast(I32), tmp[:, 2:3].bitcast(I32), EXPONENT, EXPONENT,
                                        ALU.bitwise_and, ALU.bitwise_xor)
                nc.vector.tensor_scalar(sc[:, b, 4:5].bitcast(I32), tmp[:, 2:3].bitcast(I32), EXPONENT, None, ALU.bitwise_and)
                nc.vector.tensor_scalar(sc[:, b, 1:2], tmp[:, 0:1], TOP, None, ALU.mult)
                nc.vector.tensor_scalar(tmp[:, 4:5], tmp[:, 1:2], UNTOP, cst[:, 4:5], ALU.mult, ALU.mult).then_inc(scale_step, 1)
                wait(3)
                nc.vector.tensor_scalar(sc[:, b, 3:4], tmp[:, 3:4], TOP, None, ALU.mult).then_inc(scale_step, 1)
                nc.vector.tensor_scalar(tmp[:, 5:6], sc[:, b, 1:2], cst[:, 0:1], None, ALU.mult).then_inc(scale_step, 1)
                wait(5)
                nc.vector.tensor_tensor(sc[:, b, 2:3], tmp[:, 4:5], sc[:, b, 3:4], ALU.mult).then_inc(scale_step, 1)
                nc.vector.tensor_scalar(ctxs[:, :], ctxb[:, :], tmp[:, 5:6], None, ALU.mult).then_inc(scale_step, 1)
                wait(7)
                nc.vector.tensor_copy(tmp[:, 6:7], sc[:, b, 2:3]).then_inc(x_scale, 1)

            def split_x(n, b):
                dve.wait_ge(x_hi, n + 1)
                nc.vector.scalar_tensor_tensor(out=xh[:, 1, :, 1:M + 1], in0=xf[:, :, :], scalar=sc[:, b, 1:2],
                                               in1=xh[:, 0, :, 1:M + 1], op0=ALU.mult, op1=ALU.subtract).then_inc(x_lo, 1)

            def stage_h(n, mb):
                if mb >= 2 or not (isinstance(n, int) and n == 0):
                    dve.wait_ge(h_lo, 4 * n + mb - 1)
                dve.wait_ge(conv_done, 4 * n + mb + 1)
                nc.vector.tensor_tensor(hs[:, mb % 2, :].rearrange("p (r g c) -> p r g c", r=R, g=G),
                                        C[mb % 2][:, :].rearrange("p (g r c) -> p r g c", r=R, g=G),
                                        ctxs[:, :].rearrange("p (o g c) -> p o g c", o=1, g=G).to_broadcast([P, R, G, CG]),
                                        ALU.add).then_inc(bank_free, 1)

            def split_h(n, b, mb):
                dve.wait_ge(h_hi, 4 * n + mb + 1)
                nc.vector.scalar_tensor_tensor(out=h16[:, b, 1, 4 * mb:4 * mb + 4, :].rearrange("p k c -> p (k c)"), in0=hs[:, mb % 2, :],
                                               scalar=sc[:, b, 2:3], in1=h16[:, b, 0, 4 * mb:4 * mb + 4, :].rearrange("p k c -> p (k c)"),
                                               op0=ALU.mult, op1=ALU.subtract).then_inc(h_lo, 1)

            def conv_half(n, b, half):
                for mb in (2 * half, 2 * half + 1):
                    stage_h(n, mb)
                for mb in (2 * half, 2 * half + 1):
                    split_h(n, b, mb)

            dve.wait_ge(dve_set, 12)
            max_x(0)
            scale_x(0, 0)
            split_x(0, 0)
            conv_half(0, 0, 0)
            conv_half(0, 0, 1)
            max_x(1)
            scale_x(1, 1)
            split_x(1, 1)
            for oc in range(NOC):
                for q in range(4):
                    dve.wait_ge(in_W[oc], 16 * 4)
                    ins = nc.vector.tensor_reduce(wmx[:, oc, q:q + 1], wraw(oc, 4 * q, 4), AX.X, ALU.max, apply_absolute_value=True)
                link(ins)
                nc.vector.tensor_reduce(wam[:, oc, 0:1], wmx[:, oc, :], AX.X, ALU.max).then_inc(w_max, 1)
                dve.wait_ge(w_allmax, oc + 1)
                link(nc.vector.tensor_scalar(wam[:, oc, 1:2], wam[:, oc, 1:2], FLOOR, None, ALU.max))
                link(nc.vector.tensor_scalar(wsc[:, oc, 0:1].bitcast(I32), wam[:, oc, 1:2].bitcast(I32), EXPONENT, EXPONENT,
                                             ALU.bitwise_and, ALU.bitwise_xor))
                link(nc.vector.tensor_scalar(wsc[:, oc, 1:2].bitcast(I32), wam[:, oc, 1:2].bitcast(I32), EXPONENT, None,
                                             ALU.bitwise_and))
                link(nc.vector.tensor_scalar(wsc[:, oc, 1:2], wsc[:, oc, 1:2], UNTOP, UNTOP, ALU.mult, ALU.mult))
                nc.vector.tensor_scalar(wsc[:, oc, 0:1], wsc[:, oc, 0:1], TOP, None, ALU.mult).then_inc(w_scale, 1)
                dve.wait_ge(w_scale, oc + 1)
                if oc == 0:
                    dve.wait_ge(act_set, 4 + NOC)
                nc.vector.tensor_scalar(Bp[:, oc * OC:(oc + 1) * OC], Bp[:, oc * OC:(oc + 1) * OC], wsc[:, oc, 0:1], None,
                                        ALU.mult).then_inc(dve_set, 1)
                for kb in range(KB):
                    dve.wait_ge(w_hi, oc * KB + kb + 1)
                    nc.vector.scalar_tensor_tensor(out=wslot(oc, kb, 1), in0=wraw(oc, kb), scalar=wsc[:, oc, 0:1],
                                                   in1=wslot(oc, kb, 0), op0=ALU.mult, op1=ALU.subtract).then_inc(w_lo, 1)

            def tile(t, b, conv, split):
                def wait(k):
                    dve.wait_ge(dve_sm, 5 * t + k)

                dve.wait_ge(y_free, 4 * t + NOC)
                nc.vector.tensor_scalar(yinv[:, 0:4], wsc[:, :, 1], sc[:, b, 4:5], None, ALU.mult)
                nc.vector.tensor_scalar(yinv[:, 4:5], sc[:, b, 4:5], cst[:, 7:8], UNTOP, ALU.mult, ALU.mult)
                dve.wait_ge(z_done, t + 1)
                nc.vector.tensor_copy(zs[:, ZC:2 * ZC], Z[:, ZC:2 * ZC]).then_inc(dve_sm, 1)
                wait(1)
                nc.vector.tensor_tensor(zs[:, 0:ZC], Z[:, 0:ZC], zs[:, ZC:2 * ZC], ALU.add).then_inc(dve_sm, 1)
                wait(2)
                nc.vector.scalar_tensor_tensor(out=sm[:, 0:4], in0=zs[:, ZR:ZC], scalar=yinv[:, 4:5], in1=bias4[:, :],
                                               op0=ALU.mult, op1=ALU.add).then_inc(sm_step, 1)
                dve.wait_ge(sm_step, t + 1)
                nc.vector.tensor_reduce(sm[:, 4:5], sm[:, 0:4], AX.X, ALU.max, negate=True).then_inc(dve_sm, 1)
                dve.wait_ge(act_exp, t + 1)
                nc.vector.reciprocal(sm[:, 13:14], sm[:, 12:13]).then_inc(dve_sm, 1)
                wait(4)
                nc.vector.tensor_scalar(sm[:, 16:20], sm[:, 8:12], sm[:, 13:14], cst[:, 6:7], ALU.mult, ALU.mult).then_inc(dve_sm, 1)
                wait(5)
                nc.vector.tensor_copy(zcat[:, ZR:ZR + 1], sc[:, b, 3:4])
                nc.vector.tensor_tensor(zcat[:, 0:ZR].rearrange("p (j r) -> p j r", j=EA), zs[:, 0:ZR].rearrange("p (j r) -> p j r", j=EA),
                                        sm[:, 16:20].rearrange("p (j o) -> p j o", o=1).to_broadcast([P, EA, RK]), ALU.mult).then_inc(z_ready, 1)
                if conv:
                    conv_half(t + 1, 1 - b, 0)
                    conv_half(t + 1, 1 - b, 1)
                if split:
                    max_x(t + 2)

                def leave(oc):
                    dve.wait_ge(y_done, 4 * t + oc + 1)
                    nc.vector.scalar_tensor_tensor(out=xres[:, b, oc * OC:(oc + 1) * OC], in0=Y[oc][:, :], scalar=yinv[:, oc:oc + 1],
                                                   in1=xres[:, b, oc * OC:(oc + 1) * OC], op0=ALU.mult, op1=ALU.add).then_inc(y_free, 1)

                dve.wait_ge(xr_in, 16 * (t + 1))
                leave(0)
                leave(1)
                if split:
                    scale_x(t + 2, b)
                    split_x(t + 2, b)
                leave(2)
                leave(3)

            with dve.Fori(0, N - 2, 2) as t:
                for b in range(2):
                    tile(t + b, b, True, True)
            tile(N - 2, 0, True, False)
            tile(N - 1, 1, False, False)

        @block.tensor
        def _(pe):
            pe.wait_ge(in_ctx, 48)
            pe.wait_ge(dve_set, 3)
            nc.tensor.matmul(Q[0:N, 0:P], cT_sb, cwT_sb, start=True, stop=False)
            nc.tensor.matmul(Q[0:N, 0:P], ones[:, 0:N], biasr, start=False, stop=True).then_inc(pe_set, 1)
            pe.wait_ge(dve_set, 4)
            pe.wait_ge(in_A, 32)
            for kb in range(KB):
                c = C[kb // 8][:, (kb % 8) * ZC:(kb % 8 + 1) * ZC]
                nc.tensor.matmul(c[:, 0:ZR], A_raw[:, kb * P:(kb + 1) * P], sel[:, :], start=True, stop=True)
                mm = nc.tensor.matmul(c[:, ZR:ZC], R_raw[:, kb * P:(kb + 1) * P], selr[0:E, :], start=True, stop=True)
            mm.then_inc(pe_set, 2)
            pe.wait_ge(in_B, 16)
            for oc in range(NOC):
                mm = nc.tensor.matmul(Y[oc][0:ZR, :], sel[:, :], B_raw[:, oc * OC:(oc + 1) * OC], start=True, stop=True)
            mm.then_inc(pe_set, 1)
            pe.wait_ge(dve_set, 6)
            nc.tensor.matmul(Z[:, 0:EA], rpbc, selr[0:E, :], start=True, stop=True).then_inc(pe_set, 1)
            pe.wait_ge(dve_set, 12)
            pe.wait_ge(pool_set, 4)

            def conv(n, mb):
                pe.wait_ge(bank_free, 4 * n + mb + 1)
                for g in range(G):
                    o = C[mb % 2][:, g * P:(g + 1) * P]
                    for a in range(3):
                        for xp, wp in ((0, 0), (0, 1), (1, 0)):
                            mm = nc.tensor.matmul(o, xh[:, xp, g, mb * P + 2 - a:mb * P + 2 - a + P],
                                                  T16[:, wp, g, a * P:(a + 1) * P],
                                                  start=(a == 0 and xp == 0 and wp == 0), stop=(a == 2 and xp == 1))
                mm.then_inc(conv_done, 1)

            def products(t, b, oc):
                pe.wait_ge(w_lo, KB * (oc + 1))
                if oc == 0:
                    pe.wait_ge(h_lo, 4 * (t + 1))
                pe.wait_ge(y_free, 4 * t + oc + 1)
                for kb in range(KB):
                    hh, hl = h16[:, b, 0, kb, :], h16[:, b, 1, kb, :]
                    first, last = kb == 0, kb == KB - 1
                    nc.tensor.matmul(Y[oc][:, :], hh, wslot(oc, kb, 0), start=first, stop=False)
                    nc.tensor.matmul(Y[oc][:, :], hh, wslot(oc, kb, 1), start=False, stop=False)
                    if oc == 0:
                        nc.tensor.matmul(Z[:, 0:2 * ZC], hh, A16[:, kb, :], start=first, stop=False)
                    nc.tensor.matmul(Y[oc][:, :], hl, wslot(oc, kb, 0), start=False, stop=False)
                    if oc == 0:
                        mm = nc.tensor.matmul(Z[:, 0:ZC], hl, A16[:, kb, 0:ZC], start=False, stop=last)
                if oc == 0:
                    mm.then_inc(z_done, 1)

            def lora(t, oc):
                nc.tensor.matmul(Y[oc][:, :], zT[:, :], Bp[:, oc * OC:(oc + 1) * OC], start=False, stop=True).then_inc(y_done, 1)

            pe.wait_ge(x_lo, 1)
            for mb in range(MB):
                conv(0, mb)

            def tile(t, b, more):
                products(t, b, 0)
                if more:
                    pe.wait_ge(x_lo, t + 2)
                    conv(t + 1, 0)
                    conv(t + 1, 1)
                products(t, b, 1)
                pe.wait_ge(z_ready, t + 1)
                nc.tensor.transpose(Q[:, 0:P], zcat[:, :], ident[:, :]).then_inc(z_turned, 1)
                if more:
                    conv(t + 1, 2)
                    conv(t + 1, 3)
                pe.wait_ge(zT_ready, t + 1)
                pe.wait_ge(dve_set, 12 + NOC)
                lora(t, 0)
                lora(t, 1)
                products(t, b, 2)
                lora(t, 2)
                products(t, b, 3)
                lora(t, 3)

            with pe.Fori(0, N - 2, 2) as t:
                for b in range(2):
                    tile(t + b, b, True)
            tile(N - 2, 0, True)
            tile(N - 1, 1, False)


_OUT = (N, P, L)


def kernel(**inputs):
    import numpy as np
    import concourse.bacc as bacc
    from concourse.bass_utils import run_bass_kernel_spmd as run

    i = {k: np.asarray(v) for k, v in inputs.items()}
    arrays = {
        "xc": i["x"].reshape(N, G, CG, M, R).transpose(0, 4, 2, 1, 3).reshape(N, P, G, M),
        "xr": i["x"],
        "wconv": i["L0_cond_weight"].reshape(G, CG, CG, K)[:, :, :, ::-1].transpose(2, 0, 3, 1).reshape(CG, G, K * CG),
        "condT": i["cond_128"].T,
        "cwT": i["L0_cond_c_weight"].T,
        "bias": i["fside_S_0"].reshape(1, P),
        "wt": i["L0_ffn_W_base"].reshape(NOC, OC, MB, P, R).transpose(0, 3, 2, 4, 1).reshape(NOC, P, KB * OC),
        "loraA": i["L0_ffn_lora_A"].reshape(E * RK, MB, P, R).transpose(0, 1, 3, 2).reshape(E * RK, L),
        "routerW": i["L0_ffn_router_W"].reshape(E, MB, P, R).transpose(0, 1, 3, 2).reshape(E, L),
        "loraB": i["L0_ffn_lora_B"].transpose(0, 2, 1).reshape(E * RK, O),
        "b_base": i["L0_ffn_b_base"].reshape(1, O),
        "router_b": i["L0_ffn_router_b"].reshape(E, 1),
        "prior": i["L0_ffn_domain_prior"].reshape(E, 1),
        "active": i["L0_ffn_active"].reshape(1, EA),
    }
    arrays = {k: np.ascontiguousarray(v) for k, v in arrays.items()}
    nc = bacc.Bacc("TRN2", target_bir_lowering=False, num_devices=1)
    args = [nc.dram_tensor(k, v.shape, mybir.dt.from_np(v.dtype), kind="ExternalInput").ap() for k, v in arrays.items()]
    args.append(nc.dram_tensor("out", _OUT, F32, kind="ExternalOutput").ap())
    adaln_ffn(nc, *args)
    return run(nc, [arrays], core_ids=[0]).results[0]["out"]
```

```python
from contextlib import ExitStack

import concourse.bass as bass
from concourse import mybir

ALU = mybir.AluOpType
ACT = mybir.ActivationFunctionType
AX = mybir.AxisListType
F32 = mybir.dt.float32
F16 = mybir.dt.float16
BF16 = mybir.dt.bfloat16
I32 = mybir.dt.int32
ABSMAX = bass.bass_isa.ReduceOp.absmax

P = 128
N = 32
L = 2048
O = 2048
G = 4
CG = 32
K = 9
R = 4
M = L // R
TAP = K + R - 1
OC = 512
NOC = O // OC
KB = L // P
MB = M // P
E = 16
EA = 4
RK = 8
ZR = EA * RK
ZC = ZR + EA
SCALING = 16.0 / 8.0
EPS = 1e-12
EXPONENT = 0x7F800000
TOP = 2.0 ** 13
UNTOP = 2.0 ** -14
FLOOR = 2.0 ** -40
LAG = 4
START_C = 2
START_Y = NOC
SM_STEPS = 10


def adaln_ffn(nc, xc, xr, wconv, condT, cwT, bias, wt, loraA, routerW, loraB, b_base, router_b, prior, active, out):
    ctx_rows = nc.dram_tensor("ctx_rows", (N, P), F32).ap()

    with ExitStack() as ctx:
        def sb(name, shape, dt):
            return ctx.enter_context(nc.sbuf_tensor(name, shape, dt))

        def sem(name):
            return ctx.enter_context(nc.semaphore(name))

        W16 = sb("W16", [P, (NOC * KB + LAG) * 2 * OC], F16)
        W32 = W16[:, :].bitcast(F32)
        xf = sb("xf", [P, G, M], F32)
        xh = sb("xh", [P, 2, G, M + 2], F16)
        hs = sb("hs", [P, 2, OC], F32)
        h16 = sb("h16", [P, 2, 2, KB, P], F16)
        T16 = sb("T16", [P, 2, G, TAP * CG], F16)
        A16 = sb("A16", [P, KB, 2 * ZC], F16)
        Bs = sb("Bs", [P, 2, O], BF16)
        xres = sb("xres", [P, 2, O], F32)
        ctxb = sb("ctxb", [P, P], F32)
        ctxs = sb("ctxs", [P, P], F32)
        identb = sb("identb", [P, P], BF16)
        zcat = sb("zcat", [P, 2, 2 * P], BF16)
        zT = sb("zT", [P, 2, 2 * P], BF16)
        sc = sb("sc", [P, 2, 8], F32)
        tmp = sb("tmp", [P, 8], F32)
        yinv = sb("yinv", [P, 2, 8], F32)
        cst = sb("cst", [P, 16], F32)
        cmx = sb("cmx", [P, 8], F32)
        wmx = sb("wmx", [P, NOC, 4], F32)
        wam = sb("wam", [P, NOC, 2], F32)
        wsc = sb("wsc", [P, NOC, 2], F32)
        amx = sb("amx", [P, 2], F32)
        zs = sb("zs", [P, 2 * ZC], F32)
        zr = sb("zr", [P, 2, ZR], F32)
        sm = sb("sm", [P, 24], F32)
        sel = sb("sel", [P, ZR], F32)
        selb = sb("selb", [P, ZR], BF16)
        selr = sb("selr", [P, EA], F32)
        acti = sb("acti", [P, EA], I32)
        part = sb("part", [P, 1], I32)
        actf = sb("actf", [P, 4, EA], F32)
        jrow = sb("jrow", [P, EA], F32)
        pcol = sb("pcol", [P, 1], F32)
        rbp = sb("rbp", [P, 4], F32)
        bias4 = sb("bias4", [P, EA], F32)
        braw = sb("braw", [P, 2, O // P], F32)
        bpart = sb("bpart", [P, 3, O // P], BF16)
        onesr = sb("onesr", [1, P], F32)
        biasr = sb("biasr", [1, P], F32)

        T32 = h16[:, 1, :, :, :].rearrange("p a k c -> p (a k c)").bitcast(F32)[:, 0:G * TAP * CG].rearrange("p (g c) -> p g c", g=G)
        early = h16[:, 0, :, :, :].rearrange("p a k c -> p (a k c)").bitcast(F32)
        cT_sb = early[:, 0:N]
        cwT_sb = early[:, P:2 * P]
        ctxn = early[0:N, 2 * P:3 * P]
        iot = early[:, 3 * P:4 * P]
        ioti = early[:, 4 * P:5 * P].bitcast(I32)
        rpbc = early[0:E, 5 * P:6 * P]
        late = W32[:, ((NOC - 1) * KB + LAG) * OC:(NOC * KB + LAG) * OC]
        A_raw = late[:, 0:L]
        R_raw = late[0:E, L:2 * L]
        AT32 = late[:, 2 * L:2 * L + KB * ZC].rearrange("p (k c) -> p k c", k=KB)
        BP = [late[:, 5 * L // 2 + i * O // 2:5 * L // 2 + (i + 1) * O // 2].bitcast(BF16) for i in range(3)]
        B_raw = xres[:, 1, :]
        B_rest = xres[:, 0, :]

        Y = [ctx.enter_context(nc.psum_tensor(f"Y{i}", [P, OC], F32)) for i in range(NOC)]
        C = [ctx.enter_context(nc.psum_tensor(f"C{i}", [P, OC], F32)) for i in range(2)]
        Z = ctx.enter_context(nc.psum_tensor("Z", [P, OC], F32))
        Z1 = ctx.enter_context(nc.psum_tensor("Z1", [P, OC], F32))
        Q = Z1[:, :].bitcast(BF16)

        in_act = sem("in_act")
        in_ctx = sem("in_ctx")
        in_T = sem("in_T")
        in_A = sem("in_A")
        in_B = sem("in_B")
        in_rb = sem("in_rb")
        in_b = sem("in_b")
        in_W = [[sem(f"in_W{i}_{q}") for q in range(4)] for i in range(NOC)]
        iotas = sem("iotas")
        padded = sem("padded")
        bs_zeroed = sem("bs_zeroed")
        t_zeroed = sem("t_zeroed")
        dve_link = sem("dve_link")
        sel_ready = sem("sel_ready")
        prior_ready = sem("prior_ready")
        log_ready = sem("log_ready")
        rpb_ready = sem("rpb_ready")
        bias4_made = sem("bias4_made")
        ctx_made = sem("ctx_made")
        ctx_left = sem("ctx_left")
        ctx_stored = sem("ctx_stored")
        c_max = sem("c_max")
        c_allmax = sem("c_allmax")
        c_scale = sem("c_scale")
        t_hi = sem("t_hi")
        t_lo = sem("t_lo")
        a_picked = sem("a_picked")
        a_left = sem("a_left")
        a_max = sem("a_max")
        a_allmax = sem("a_allmax")
        a_scale = sem("a_scale")
        a_hi = sem("a_hi")
        a_lo = sem("a_lo")
        b_part = sem("b_part")
        b_rest = sem("b_rest")
        bias_part = sem("bias_part")
        bias_rows = sem("bias_rows")
        b_picked = sem("b_picked")
        b_left = sem("b_left")
        b_scaled = sem("b_scaled")
        w_max = sem("w_max")
        w_allmax = sem("w_allmax")
        w_scale = sem("w_scale")
        w_hi = sem("w_hi")
        w_lo = sem("w_lo")
        x_in = sem("x_in")
        c_in = sem("c_in")
        xr_in = [sem("xr_in0"), sem("xr_in1")]
        x_max = sem("x_max")
        x_allmax = sem("x_allmax")
        max_seen = sem("max_seen")
        scale_step = sem("scale_step")
        x_scale = sem("x_scale")
        x_hi = sem("x_hi")
        x_lo = sem("x_lo")
        conv_done = sem("conv_done")
        bank_free = sem("bank_free")
        h_hi = sem("h_hi")
        h_lo = sem("h_lo")
        z_done = sem("z_done")
        sm_step = sem("sm_step")
        sm_exp = sem("sm_exp")
        z_ready = sem("z_ready")
        z_turned = sem("z_turned")
        zT_ready = sem("zT_ready")
        y_done = sem("y_done")
        y_free = sem("y_free")
        out_done = sem("out_done")

        block = ctx.enter_context(nc.Block())

        FIRST = [(0, 0), (1, 0), (0, 1), (1, 1), (0, 2), (1, 2), (0, 3), (1, 3)]
        FIRST_BANK = {(0, 0): Y[0], (1, 0): C[0], (0, 1): Y[1], (1, 1): C[1], (0, 2): Y[2], (1, 2): C[0], (0, 3): Y[3], (1, 3): Y[3]}

        def wslot(oc, kb, half):
            at = ((oc * KB + kb) * 2 + half) * OC
            return W16[:, at:at + OC]

        def wraw(oc, kb, n=1):
            at = (oc * KB + kb + LAG) * OC
            return W32[:, at:at + n * OC]

        @block.sync
        def _(sp):
            def load_ctx(n):
                row = ctx_rows[n:n + 1, :] if isinstance(n, int) else ctx_rows[bass.ds(n, 1), :]
                sp.dma_start(ctxb[:, :], row.partition_broadcast(P)).then_inc(c_in, 16)

            def load_x(n):
                sp.wait_ge(x_hi, n)
                sp.wait_ge(x_lo, n)
                sp.dma_start(xf[:, :, :], xc[n]).then_inc(x_in, 16)
                load_ctx(n)

            def load_res(n, b):
                sp.dma_start(xres[:, b, :], xr[n]).then_inc(xr_in[b], 16)

            def load_w(oc):
                for q in range(4):
                    sp.dma_start(wraw(oc, 4 * q, 4), wt[oc, :, q * 4 * OC:(q + 1) * 4 * OC]).then_inc(in_W[oc][q], 16)

            sp.dma_start(xf[:, :, :], xc[0]).then_inc(x_in, 16)
            sp.wait_ge(t_zeroed, 1)
            for r in range(R):
                sp.dma_start(T32[r * CG:(r + 1) * CG, :, r * CG:(r + K) * CG], wconv).then_inc(in_T, 16)
            sp.dma_start(A_raw, loraA).then_inc(in_A, 16)
            sp.dma_start(R_raw, routerW).then_inc(in_A, 16)
            sp.wait_ge(ctx_stored, 16)
            load_ctx(0)
            load_w(0)
            sp.dma_start(B_raw, loraB).then_inc(in_B, 16)
            load_x(1)
            load_w(1)
            load_w(2)
            load_x(2)
            sp.wait_ge(a_lo, 2)
            sp.wait_ge(b_picked, NOC)
            load_w(3)
            sp.wait_ge(b_rest, 2)
            load_res(0, 0)
            load_res(1, 1)

            def store(t, b, oc, left):
                sp.wait_ge(y_free, left + START_Y)
                sp.dma_start(out[t, :, oc * OC:(oc + 1) * OC], xres[:, b, oc * OC:(oc + 1) * OC]).then_inc(out_done, 16)

            for i, (t, oc) in enumerate(FIRST):
                if i == 6:
                    load_x(3)
                store(t, t, oc, i + 1)
            load_x(4)
            sp.wait_ge(out_done, 16 * len(FIRST))
            load_res(2, 0)
            load_res(3, 1)

            def tile(t, b, more_x, more_res):
                store(t, b, 0, 4 * t + 1)
                store(t, b, 1, 4 * t + 2)
                if more_x:
                    load_x(t + 3)
                store(t, b, 2, 4 * t + 3)
                store(t, b, 3, 4 * t + 4)
                if more_res:
                    sp.wait_ge(out_done, 64 * (t + 1))
                    load_res(t + 2, b)

            with sp.Fori(2, N - 4, 2) as t:
                for b in range(2):
                    tile(t + b, b, True, True)
            tile(N - 4, 0, True, True)
            for t in range(N - 3, N):
                tile(t, t % 2, False, t < N - 2)
            sp.wait_ge(out_done, 64 * N)

        @block.gpsimd
        def _(pool):
            nc.gpsimd.iota(ioti, [[1, P]], base=0, channel_multiplier=0).then_inc(iotas, 1)
            nc.gpsimd.iota(part[:, :], [[0, 1]], base=0, channel_multiplier=1).then_inc(iotas, 1)
            nc.gpsimd.memset(onesr[:, :], 1.0).then_inc(padded, 1)
            nc.gpsimd.memset(xh[:, :, :, 0:1], 0.0).then_inc(padded, 1)
            nc.gpsimd.memset(xh[:, :, :, M + 1:M + 2], 0.0).then_inc(padded, 1)
            nc.gpsimd.memset(zcat[:, :, :], 0.0).then_inc(padded, 1)
            pool.wait_ge(padded, 4)
            nc.gpsimd.memset(Bs[ZR * 2:P, 1, :], 0.0).then_inc(bs_zeroed, 1)
            pool.wait_ge(bs_zeroed, 1)
            pool.wait_ge(x_max, 1)
            nc.gpsimd.partition_all_reduce(amx[:, 1:2], amx[:, 0:1], P, ABSMAX).then_inc(x_allmax, 1)
            pool.wait_ge(c_max, 1)
            nc.gpsimd.partition_all_reduce(cmx[:, 4:6], cmx[:, 0:2], P, ABSMAX).then_inc(c_allmax, 1)
            pool.wait_ge(a_max, 1)
            nc.gpsimd.partition_all_reduce(cmx[:, 6:8], cmx[:, 2:4], P, ABSMAX).then_inc(a_allmax, 1)
            pool.wait_ge(x_max, 2)
            nc.gpsimd.partition_all_reduce(amx[:, 1:2], amx[:, 0:1], P, ABSMAX).then_inc(x_allmax, 1)
            for oc in range(NOC):
                pool.wait_ge(w_max, oc + 1)
                nc.gpsimd.partition_all_reduce(wam[:, oc, 1:2], wam[:, oc, 0:1], P, ABSMAX).then_inc(w_allmax, 1)

            with pool.Fori(2, N, 1) as n:
                pool.wait_ge(x_max, n + 1)
                pool.sem_inc(max_seen, 1)
                nc.gpsimd.partition_all_reduce(amx[:, 1:2], amx[:, 0:1], P, ABSMAX).then_inc(x_allmax, 1)

        @block.scalar
        def _(act):
            act.dma_start(cT_sb, condT).then_inc(in_ctx, 16)
            act.dma_start(cwT_sb, cwT).then_inc(in_ctx, 16)
            act.dma_start(biasr[:, :], bias).then_inc(in_ctx, 16)
            act.dma_start(acti[:, :], active.partition_broadcast(P)).then_inc(in_act, 16)
            act.dma_start(rbp[0:E, 0:1], router_b).then_inc(in_rb, 16)
            act.dma_start(rbp[0:E, 1:2], prior).then_inc(in_rb, 16)
            act.dma_start(braw[:, 0, :], b_base).then_inc(in_b, 16)
            act.wait_ge(ctx_made, 1)
            nc.scalar.copy(ctxn, Z[0:N, 0:P]).then_inc(ctx_left, 1)
            act.wait_ge(ctx_left, 1)
            act.dma_start(ctx_rows, ctxn).then_inc(ctx_stored, 16)
            act.wait_ge(prior_ready, 1)
            nc.scalar.activation(rbp[0:E, 2:3], rbp[0:E, 1:2], ACT.Ln).then_inc(log_ready, 1)

            def split_x(n, b):
                act.wait_ge(x_scale, n + 1)
                nc.scalar.activation(xh[:, 0, :, 1:M + 1], xf[:, :, :], ACT.Copy, scale=sc[:, b, 1:2]).then_inc(x_hi, 1)

            def split_h(n, b, mb):
                act.wait_ge(bank_free, 4 * n + mb + 1 + START_C)
                nc.scalar.activation(h16[:, b, 0, 4 * mb:4 * mb + 4, :].rearrange("p k c -> p (k c)"), hs[:, mb % 2, :],
                                     ACT.Copy, scale=sc[:, b, 2:3]).then_inc(h_hi, 1)

            def split_w(oc, kbs):
                act.wait_ge(w_scale, oc + 1)
                for kb in kbs:
                    if oc * KB + kb >= LAG:
                        act.wait_ge(w_lo, oc * KB + kb - LAG + 1)
                    nc.scalar.activation(wslot(oc, kb, 0), wraw(oc, kb), ACT.Copy, scale=wsc[:, oc, 0:1]).then_inc(w_hi, 1)

            def exp(t):
                act.wait_ge(sm_step, SM_STEPS * t + 4)
                nc.scalar.activation(sm[:, 8:12], sm[:, 0:4], ACT.Exp, bias=sm[:, 4:5], accum_out=sm[:, 12:13]).then_inc(sm_exp, 1)

            def copy_zT(t, b, turned):
                act.wait_ge(z_turned, turned)
                nc.scalar.copy(zT[:, b, :], Q[:, b * 2 * P:(b + 1) * 2 * P]).then_inc(zT_ready, 1)

            act.wait_ge(c_scale, 1)
            nc.scalar.activation(T16[:, 0, :, :], T32, ACT.Copy, scale=cst[:, 0:1]).then_inc(t_hi, 1)
            split_x(0, 0)
            act.wait_ge(a_picked, 1)
            for i in range(2):
                nc.scalar.copy(AT32[:, i * KB // 2:(i + 1) * KB // 2, :],
                               Y[i][:, 0:KB // 2 * ZC].rearrange("p (k c) -> p k c", c=ZC)).then_inc(a_left, 1)
            act.wait_ge(ctx_stored, 16)
            act.wait_ge(bias4_made, 1)
            for mb in range(MB):
                split_h(0, 0, mb)
            act.wait_ge(a_scale, 1)
            nc.scalar.activation(A16[:, :, 0:ZR], AT32[:, :, 0:ZR], ACT.Copy, scale=cst[:, 2:3]).then_inc(a_hi, 1)
            nc.scalar.activation(A16[:, :, ZR:ZC], AT32[:, :, ZR:ZC], ACT.Copy, scale=cst[:, 3:4]).then_inc(a_hi, 1)
            act.wait_ge(in_B, 16)
            nc.scalar.copy(BP[0], B_raw).then_inc(b_part, 1)
            split_x(1, 1)
            act.wait_ge(b_rest, 1)
            nc.scalar.copy(BP[1], B_rest).then_inc(b_part, 1)
            act.wait_ge(t_lo, 1)
            for mb in range(MB):
                split_h(1, 1, mb)
            for oc in range(NOC):
                act.wait_ge(b_picked, oc + 1)
                o = slice(oc * OC, (oc + 1) * OC)
                nc.scalar.mul(Bs[:, 0, o], Y[2 - 2 * (oc % 2)][:, :], SCALING).then_inc(b_left, 1)
                nc.scalar.mul(Bs[0:2 * ZR, 1, o], Y[3 - 2 * (oc % 2)][0:2 * ZR, :], SCALING).then_inc(b_left, 1)
            act.wait_ge(bias_part, 1)
            act.wait_ge(bs_zeroed, 1)
            for i in range(3):
                act.dma_start(Bs[2 * ZR + i:2 * ZR + i + 1, 1, :], bpart[:, i, :]).then_inc(bias_rows, 16)
            split_w(0, range(KB))
            split_w(1, range(KB))
            exp(0)
            exp(1)
            split_w(2, range(KB // 2))
            copy_zT(0, 0, 2)
            copy_zT(1, 1, 2)
            split_w(2, range(KB // 2, KB))
            split_w(3, range(KB))
            split_x(2, 0)
            for mb in range(MB):
                split_h(2, 0, mb)
            split_x(3, 1)

            def tile(t, b, conv, split):
                exp(t)
                if conv:
                    split_h(t + 1, 1 - b, 0)
                    split_h(t + 1, 1 - b, 1)
                copy_zT(t, b, t + 1)
                if conv:
                    split_h(t + 1, 1 - b, 2)
                    split_h(t + 1, 1 - b, 3)
                if split:
                    split_x(t + 2, b)

            with act.Fori(2, N - 2, 2) as t:
                for b in range(2):
                    tile(t + b, b, True, True)
            tile(N - 2, 0, True, False)
            tile(N - 1, 1, False, False)

        @block.vector
        def _(dve):
            step = [0]

            def link(ins):
                step[0] += 1
                ins.then_inc(dve_link, 1)
                dve.wait_ge(dve_link, step[0])

            nc.vector.memset(T32, 0.0).then_inc(t_zeroed, 1)
            nc.vector.memset(cmx[:, :], FLOOR).then_inc(y_free, START_Y)
            nc.vector.memset(tmp[:, :], 0.0).then_inc(bank_free, START_C)
            dve.wait_ge(in_act, 16)
            link(nc.vector.tensor_copy(actf[:, 0, :], acti[:, :]))
            link(nc.vector.tensor_scalar(actf[:, 1, :], actf[:, 0, :], 0.0, float(E), ALU.is_lt, ALU.mult))
            link(nc.vector.tensor_tensor(actf[:, 2, :], actf[:, 0, :], actf[:, 1, :], ALU.add))
            link(nc.vector.tensor_scalar(actf[:, 3, :], actf[:, 2, :], 0.0, float(E - 1), ALU.max, ALU.min))
            dve.wait_ge(iotas, 2)
            link(nc.vector.tensor_scalar(jrow[:, :], actf[:, 3, :], float(RK), None, ALU.mult))
            nc.vector.tensor_copy(iot, ioti)
            link(nc.vector.tensor_copy(pcol[:, :], part[:, :]))
            for j in range(EA):
                ins = nc.vector.tensor_scalar(sel[:, RK * j:RK * j + RK], iot[:, 0:RK], jrow[:, j:j + 1], None, ALU.add)
            link(ins)
            link(nc.vector.tensor_scalar(sel[:, :], sel[:, :], pcol[:, 0:1], None, ALU.is_equal))
            nc.vector.tensor_copy(selb[:, :], sel[:, :])
            nc.vector.tensor_scalar(identb[:, :], iot, pcol[:, 0:1], None, ALU.is_equal)
            nc.vector.tensor_scalar(selr[:, :], actf[:, 3, :], pcol[:, 0:1], None, ALU.is_equal).then_inc(sel_ready, 1)
            dve.wait_ge(in_rb, 32)
            nc.vector.tensor_scalar(rbp[0:E, 1:2], rbp[0:E, 1:2], EPS, None, ALU.add).then_inc(prior_ready, 1)

            def max_x(n):
                dve.wait_ge(x_in, 16 * (n + 1))
                nc.vector.tensor_reduce(amx[:, 0:1], xf[:, :, :], AX.XY, ALU.max, apply_absolute_value=True).then_inc(x_max, 1)

            SCALE_STEPS = 7

            def scale_x(n, b):
                def wait(k):
                    dve.wait_ge(scale_step, SCALE_STEPS * n + k)

                if not (isinstance(n, int) and n == 0):
                    dve.wait_ge(h_lo, 4 * n)
                dve.wait_ge(x_allmax, n + 1)
                nc.vector.tensor_scalar(sc[:, b, 0:1], amx[:, 1:2], FLOOR, None, ALU.max).then_inc(scale_step, 1)
                wait(1)
                nc.vector.tensor_scalar(tmp[:, 0:1].bitcast(I32), sc[:, b, 0:1].bitcast(I32), EXPONENT, EXPONENT,
                                        ALU.bitwise_and, ALU.bitwise_xor)
                nc.vector.tensor_scalar(tmp[:, 1:2].bitcast(I32), sc[:, b, 0:1].bitcast(I32), EXPONENT, None, ALU.bitwise_and)
                nc.vector.tensor_scalar(tmp[:, 2:3], sc[:, b, 0:1], cst[:, 8:9], cst[:, 9:10], ALU.mult, ALU.add).then_inc(scale_step, 1)
                wait(2)
                nc.vector.tensor_scalar(tmp[:, 3:4].bitcast(I32), tmp[:, 2:3].bitcast(I32), EXPONENT, EXPONENT,
                                        ALU.bitwise_and, ALU.bitwise_xor)
                nc.vector.tensor_scalar(sc[:, b, 4:5].bitcast(I32), tmp[:, 2:3].bitcast(I32), EXPONENT, None, ALU.bitwise_and)
                nc.vector.tensor_scalar(sc[:, b, 1:2], tmp[:, 0:1], TOP, None, ALU.mult)
                nc.vector.tensor_scalar(tmp[:, 4:5], tmp[:, 1:2], UNTOP, cst[:, 4:5], ALU.mult, ALU.mult).then_inc(scale_step, 1)
                wait(3)
                nc.vector.tensor_scalar(sc[:, b, 3:4], tmp[:, 3:4], TOP, None, ALU.mult).then_inc(scale_step, 1)
                nc.vector.tensor_scalar(tmp[:, 5:6], sc[:, b, 1:2], cst[:, 0:1], None, ALU.mult).then_inc(scale_step, 1)
                wait(5)
                dve.wait_ge(c_in, 16 * (n + 1))
                nc.vector.tensor_tensor(sc[:, b, 2:3], tmp[:, 4:5], sc[:, b, 3:4], ALU.mult).then_inc(scale_step, 1)
                nc.vector.tensor_scalar(ctxs[:, :], ctxb[:, :], tmp[:, 5:6], None, ALU.mult).then_inc(scale_step, 1)
                wait(7)
                nc.vector.tensor_copy(tmp[:, 6:7], sc[:, b, 2:3]).then_inc(x_scale, 1)

            def split_x(n, b):
                dve.wait_ge(x_hi, n + 1)
                nc.vector.scalar_tensor_tensor(out=xh[:, 1, :, 1:M + 1], in0=xf[:, :, :], scalar=sc[:, b, 1:2],
                                               in1=xh[:, 0, :, 1:M + 1], op0=ALU.mult, op1=ALU.subtract).then_inc(x_lo, 1)

            def stage_h(n, mb):
                if mb >= 2 or not (isinstance(n, int) and n == 0):
                    dve.wait_ge(h_lo, 4 * n + mb - 1)
                dve.wait_ge(conv_done, 4 * n + mb + 1)
                nc.vector.tensor_tensor(hs[:, mb % 2, :].rearrange("p (r g c) -> p r g c", r=R, g=G),
                                        C[mb % 2][:, :].rearrange("p (g r c) -> p r g c", r=R, g=G),
                                        ctxs[:, :].rearrange("p (o g c) -> p o g c", o=1, g=G).to_broadcast([P, R, G, CG]),
                                        ALU.add).then_inc(bank_free, 1)

            def split_h(n, b, mb):
                dve.wait_ge(h_hi, 4 * n + mb + 1)
                nc.vector.scalar_tensor_tensor(out=h16[:, b, 1, 4 * mb:4 * mb + 4, :].rearrange("p k c -> p (k c)"), in0=hs[:, mb % 2, :],
                                               scalar=sc[:, b, 2:3], in1=h16[:, b, 0, 4 * mb:4 * mb + 4, :].rearrange("p k c -> p (k c)"),
                                               op0=ALU.mult, op1=ALU.subtract).then_inc(h_lo, 1)

            def conv_half(n, b, half):
                for mb in (2 * half, 2 * half + 1):
                    stage_h(n, mb)
                for mb in (2 * half, 2 * half + 1):
                    split_h(n, b, mb)

            def make_scales(lo, hi):
                link(nc.vector.tensor_scalar(cmx[:, 4 + lo:4 + hi], cmx[:, 4 + lo:4 + hi], FLOOR, None, ALU.max))
                nc.vector.tensor_scalar(cst[:, lo:hi].bitcast(I32), cmx[:, 4 + lo:4 + hi].bitcast(I32), EXPONENT, EXPONENT,
                                        ALU.bitwise_and, ALU.bitwise_xor)
                link(nc.vector.tensor_scalar(cst[:, 4 + lo:4 + hi].bitcast(I32), cmx[:, 4 + lo:4 + hi].bitcast(I32), EXPONENT, None,
                                             ALU.bitwise_and))
                nc.vector.tensor_scalar(cst[:, 4 + lo:4 + hi], cst[:, 4 + lo:4 + hi], UNTOP, None, ALU.mult)
                if lo == 0:
                    nc.vector.tensor_scalar(cst[:, 8:9], cmx[:, 4:5], float(K * CG), None, ALU.mult)
                    nc.vector.tensor_copy(cst[:, 9:10], cmx[:, 5:6])
                return nc.vector.tensor_scalar(cst[:, lo:hi], cst[:, lo:hi], TOP, None, ALU.mult)

            def prepare_w(oc):
                for q in range(4):
                    dve.wait_ge(in_W[oc][q], 16)
                    ins = nc.vector.tensor_reduce(wmx[:, oc, q:q + 1], wraw(oc, 4 * q, 4), AX.X, ALU.max, apply_absolute_value=True)
                link(ins)
                nc.vector.tensor_reduce(wam[:, oc, 0:1], wmx[:, oc, :], AX.X, ALU.max).then_inc(w_max, 1)
                dve.wait_ge(w_allmax, oc + 1)
                link(nc.vector.tensor_scalar(wam[:, oc, 1:2], wam[:, oc, 1:2], FLOOR, None, ALU.max))
                nc.vector.tensor_scalar(wsc[:, oc, 0:1].bitcast(I32), wam[:, oc, 1:2].bitcast(I32), EXPONENT, EXPONENT,
                                        ALU.bitwise_and, ALU.bitwise_xor)
                link(nc.vector.tensor_scalar(wsc[:, oc, 1:2].bitcast(I32), wam[:, oc, 1:2].bitcast(I32), EXPONENT, None,
                                             ALU.bitwise_and))
                nc.vector.tensor_scalar(wsc[:, oc, 1:2], wsc[:, oc, 1:2], UNTOP, UNTOP, ALU.mult, ALU.mult)
                nc.vector.tensor_scalar(wsc[:, oc, 0:1], wsc[:, oc, 0:1], TOP, None, ALU.mult).then_inc(w_scale, 1)
                dve.wait_ge(w_scale, oc + 1)
                for kb in range(KB):
                    dve.wait_ge(w_hi, oc * KB + kb + 1)
                    nc.vector.scalar_tensor_tensor(out=wslot(oc, kb, 1), in0=wraw(oc, kb), scalar=wsc[:, oc, 0:1],
                                                   in1=wslot(oc, kb, 0), op0=ALU.mult, op1=ALU.subtract).then_inc(w_lo, 1)
                dve.wait_ge(b_left, 2 * NOC)
                dve.wait_ge(bias_rows, 48)
                nc.vector.tensor_scalar(Bs[:, :, oc * OC:(oc + 1) * OC], Bs[:, :, oc * OC:(oc + 1) * OC], wsc[:, oc, 0:1], None,
                                        ALU.mult).then_inc(b_scaled, 1)

            max_x(0)
            dve.wait_ge(ctx_left, 1)
            nc.vector.tensor_reduce(cmx[0:N, 1:2], ctxn, AX.X, ALU.max, apply_absolute_value=True)
            dve.wait_ge(in_T, 16 * R)
            nc.vector.tensor_reduce(cmx[:, 0:1], T32, AX.XY, ALU.max, apply_absolute_value=True).then_inc(c_max, 1)
            dve.wait_ge(log_ready, 1)
            link(nc.vector.tensor_tensor(rbp[0:E, 3:4], rbp[0:E, 2:3], rbp[0:E, 0:1], ALU.add))
            link(nc.vector.memset(rpbc, 0.0))
            nc.vector.tensor_scalar(rpbc, rpbc, rbp[0:E, 3:4], None, ALU.add).then_inc(rpb_ready, 1)
            dve.wait_ge(c_allmax, 1)
            make_scales(0, 2).then_inc(c_scale, 1)
            dve.wait_ge(c_scale, 1)
            scale_x(0, 0)
            dve.wait_ge(t_hi, 1)
            nc.vector.scalar_tensor_tensor(out=T16[:, 1, :, :], in0=T32, scalar=cst[:, 0:1],
                                           in1=T16[:, 0, :, :], op0=ALU.mult, op1=ALU.subtract).then_inc(t_lo, 1)
            split_x(0, 0)
            dve.wait_ge(a_left, 2)
            nc.vector.tensor_reduce(cmx[:, 2:3], AT32[:, :, 0:ZR], AX.XY, ALU.max, apply_absolute_value=True)
            nc.vector.tensor_reduce(cmx[:, 3:4], AT32[:, :, ZR:ZC], AX.XY, ALU.max, apply_absolute_value=True).then_inc(a_max, 1)
            dve.wait_ge(in_b, 16)
            link(nc.vector.tensor_copy(bpart[:, 0, :], braw[:, 0, :]))
            link(nc.vector.tensor_tensor(braw[:, 1, :], braw[:, 0, :], bpart[:, 0, :], ALU.subtract))
            link(nc.vector.tensor_copy(bpart[:, 1, :], braw[:, 1, :]))
            nc.vector.tensor_tensor(bpart[:, 2, :], braw[:, 1, :], bpart[:, 1, :], ALU.subtract).then_inc(bias_part, 1)
            dve.wait_ge(a_allmax, 1)
            make_scales(2, 4).then_inc(a_scale, 1)
            dve.wait_ge(a_scale, 1)
            dve.wait_ge(bias4_made, 1)
            nc.vector.tensor_copy(bias4[:, :], Z[:, 0:EA])
            conv_half(0, 0, 0)
            conv_half(0, 0, 1)
            dve.wait_ge(a_hi, 2)
            nc.vector.scalar_tensor_tensor(out=A16[:, :, ZC:ZC + ZR], in0=AT32[:, :, 0:ZR], scalar=cst[:, 2:3],
                                           in1=A16[:, :, 0:ZR], op0=ALU.mult, op1=ALU.subtract).then_inc(a_lo, 1)
            nc.vector.scalar_tensor_tensor(out=A16[:, :, ZC + ZR:2 * ZC], in0=AT32[:, :, ZR:ZC], scalar=cst[:, 3:4],
                                           in1=A16[:, :, ZR:ZC], op0=ALU.mult, op1=ALU.subtract).then_inc(a_lo, 1)
            max_x(1)
            scale_x(1, 1)
            split_x(1, 1)
            dve.wait_ge(b_part, 1)
            nc.vector.tensor_tensor(B_rest, B_raw, BP[0], ALU.subtract).then_inc(b_rest, 1)
            dve.wait_ge(b_part, 2)
            nc.vector.tensor_tensor(BP[2], B_rest, BP[1], ALU.subtract).then_inc(b_rest, 1)
            conv_half(1, 1, 0)
            conv_half(1, 1, 1)

            def softmax(t, b, bank=Z):
                def wait(k):
                    dve.wait_ge(sm_step, SM_STEPS * t + k)

                if not (isinstance(t, int) and t == 0):
                    dve.wait_ge(z_ready, t)
                dve.wait_ge(z_done, t + 1)
                nc.vector.tensor_scalar(yinv[:, b, 4:5], sc[:, b, 4:5], cst[:, 7:8], UNTOP, ALU.mult, ALU.mult)
                zb = bank[:, 0:2 * ZC]
                nc.vector.tensor_copy(zs[:, ZC:2 * ZC], zb[:, ZC:2 * ZC]).then_inc(sm_step, 1)
                wait(1)
                nc.vector.tensor_tensor(zs[:, 0:ZC], zb[:, 0:ZC], zs[:, ZC:2 * ZC], ALU.add).then_inc(sm_step, 1)
                wait(2)
                nc.vector.scalar_tensor_tensor(out=sm[:, 0:4], in0=zs[:, ZR:ZC], scalar=yinv[:, b, 4:5], in1=bias4[:, :],
                                               op0=ALU.mult, op1=ALU.add).then_inc(sm_step, 1)
                wait(3)
                nc.vector.tensor_reduce(sm[:, 4:5], sm[:, 0:4], AX.X, ALU.max, negate=True).then_inc(sm_step, 1)
                dve.wait_ge(sm_exp, t + 1)
                nc.vector.reciprocal(sm[:, 13:14], sm[:, 12:13]).then_inc(sm_step, 1)
                wait(5)
                nc.vector.tensor_scalar(sm[:, 16:20], sm[:, 8:12], sm[:, 13:14], cst[:, 6:7], ALU.mult, ALU.mult).then_inc(sm_step, 1)
                wait(6)
                nc.vector.tensor_tensor(zr[:, 0, :].rearrange("p (j r) -> p j r", j=EA), zs[:, 0:ZR].rearrange("p (j r) -> p j r", j=EA),
                                        sm[:, 16:20].rearrange("p (j o) -> p j o", o=1).to_broadcast([P, EA, RK]), ALU.mult).then_inc(sm_step, 1)
                wait(7)

                def put(at, n, src):
                    return nc.vector.tensor_copy(zcat[:, b, at:at + n * ZR].rearrange("p (n c) -> p n c", n=n),
                                                 src.rearrange("p (o c) -> p o c", o=1).to_broadcast([P, n, ZR]))

                put(0, 3, zr[:, 0, :]).then_inc(sm_step, 1)
                wait(8)
                nc.vector.tensor_tensor(zr[:, 1, :], zr[:, 0, :], zcat[:, b, 0:ZR], ALU.subtract).then_inc(sm_step, 1)
                wait(9)
                put(3 * ZR, 2, zr[:, 1, :]).then_inc(sm_step, 1)
                wait(10)
                nc.vector.tensor_copy(zcat[:, b, 6 * ZR:6 * ZR + 3], sc[:, b, 3:4].to_broadcast([P, 3]))
                nc.vector.tensor_tensor(zcat[:, b, 5 * ZR:6 * ZR], zr[:, 1, :], zcat[:, b, 3 * ZR:4 * ZR], ALU.subtract).then_inc(z_ready, 1)

            def leave(t, b, oc, bank, done):
                dve.wait_ge(y_done, done)
                nc.vector.scalar_tensor_tensor(out=xres[:, b, oc * OC:(oc + 1) * OC], in0=bank[:, :], scalar=yinv[:, b, oc:oc + 1],
                                               in1=xres[:, b, oc * OC:(oc + 1) * OC], op0=ALU.mult, op1=ALU.add).then_inc(y_free, 1)

            def first(i):
                t, oc = FIRST[i]
                link(nc.vector.tensor_scalar(yinv[:, t, oc:oc + 1], wsc[:, oc, 1:2], sc[:, t, 4:5], None, ALU.mult))
                leave(t, t, oc, FIRST_BANK[t, oc], i + 1)

            dve.wait_ge(padded, 4)
            prepare_w(0)
            prepare_w(1)
            softmax(0, 0)
            softmax(1, 1, Z1)
            prepare_w(2)
            dve.wait_ge(xr_in[0], 16)
            dve.wait_ge(xr_in[1], 16)
            for i in range(4):
                first(i)
            prepare_w(3)
            for t in range(2):
                nc.vector.tensor_scalar(yinv[:, t, 5:6], sc[:, t, 4:5], wsc[:, 3, 1:2], None, ALU.mult)
            first(4)
            first(5)
            max_x(2)
            link(nc.vector.tensor_copy(yinv[:, 0, 3:4], yinv[:, 0, 5:6]))
            link(nc.vector.tensor_copy(yinv[:, 1, 3:4], yinv[:, 1, 5:6]))
            scale_x(2, 0)
            split_x(2, 0)
            leave(0, 0, 3, FIRST_BANK[0, 3], 7)
            conv_half(2, 0, 0)
            conv_half(2, 0, 1)
            max_x(3)
            scale_x(3, 1)
            split_x(3, 1)
            leave(1, 1, 3, FIRST_BANK[1, 3], 8)

            def tile(t, b, conv, split):
                dve.wait_ge(y_free, 4 * t + START_Y)
                nc.vector.tensor_scalar(yinv[:, b, 0:4], wsc[:, :, 1], sc[:, b, 4:5], None, ALU.mult)
                softmax(t, b)
                if conv:
                    conv_half(t + 1, 1 - b, 0)
                    conv_half(t + 1, 1 - b, 1)
                if split:
                    max_x(t + 2)
                dve.wait_ge(xr_in[b], 8 * (t - b) + 16)
                leave(t, b, 0, Y[0], 4 * t + 1)
                leave(t, b, 1, Y[1], 4 * t + 2)
                if split:
                    scale_x(t + 2, b)
                    split_x(t + 2, b)
                leave(t, b, 2, Y[2], 4 * t + 3)
                leave(t, b, 3, Y[3], 4 * t + 4)

            with dve.Fori(2, N - 2, 2) as t:
                for b in range(2):
                    tile(t + b, b, True, True)
            tile(N - 2, 0, True, False)
            tile(N - 1, 1, False, False)

        @block.tensor
        def _(pe):
            def conv(n, mb, free):
                pe.wait_ge(bank_free, free)
                for g in range(G):
                    o = C[mb % 2][:, g * P:(g + 1) * P]
                    for a in range(3):
                        for xp, wp in ((0, 0), (0, 1), (1, 0)):
                            mm = nc.tensor.matmul(o, xh[:, xp, g, mb * P + 2 - a:mb * P + 2 - a + P],
                                                  T16[:, wp, g, a * P:(a + 1) * P],
                                                  start=(a == 0 and xp == 0 and wp == 0), stop=(a == 2 and xp == 1))
                mm.then_inc(conv_done, 1)

            def products(b, oc, bank, fresh=False, zbank=Z):
                zb = zbank[:, 0:2 * ZC]
                for kb in range(KB):
                    if fresh:
                        pe.wait_ge(w_lo, oc * KB + kb + 1)
                    hh, hl = h16[:, b, 0, kb, :], h16[:, b, 1, kb, :]
                    first, last = kb == 0, kb == KB - 1
                    nc.tensor.matmul(bank[:, :], hh, wslot(oc, kb, 0), start=first, stop=False)
                    nc.tensor.matmul(bank[:, :], hh, wslot(oc, kb, 1), start=False, stop=False)
                    if oc == 0:
                        nc.tensor.matmul(zb, hh, A16[:, kb, :], start=first, stop=False)
                    nc.tensor.matmul(bank[:, :], hl, wslot(oc, kb, 0), start=False, stop=False)
                    if oc == 0:
                        mm = nc.tensor.matmul(zb[:, 0:ZC], hl, A16[:, kb, 0:ZC], start=False, stop=last)
                if oc == 0:
                    mm.then_inc(z_done, 1)

            def turn(t, b, ready):
                pe.wait_ge(z_ready, ready)
                for i in range(2):
                    mm = nc.tensor.transpose(Q[:, (2 * b + i) * P:(2 * b + i + 1) * P], zcat[:, b, i * P:(i + 1) * P], identb[:, :])
                mm.then_inc(z_turned, 1)

            def lora(b, oc, bank):
                nc.tensor.matmul(bank[:, :], zT[:, b, 0:P], Bs[:, 0, oc * OC:(oc + 1) * OC], start=False, stop=False)
                nc.tensor.matmul(bank[:, :], zT[:, b, P:2 * P], Bs[:, 1, oc * OC:(oc + 1) * OC], start=False, stop=True).then_inc(y_done, 1)

            pe.wait_ge(in_ctx, 48)
            pe.wait_ge(padded, 1)
            nc.tensor.matmul(Z[0:N, 0:P], cT_sb, cwT_sb, start=True, stop=False)
            nc.tensor.matmul(Z[0:N, 0:P], onesr[:, 0:N], biasr[:, :], start=False, stop=True).then_inc(ctx_made, 1)
            pe.wait_ge(sel_ready, 1)
            pe.wait_ge(in_A, 32)
            for kb in range(KB):
                c = Y[kb // 8][:, (kb % 8) * ZC:(kb % 8 + 1) * ZC]
                nc.tensor.matmul(c[:, 0:ZR], A_raw[:, kb * P:(kb + 1) * P], sel[:, :], start=True, stop=True)
                mm = nc.tensor.matmul(c[:, ZR:ZC], R_raw[:, kb * P:(kb + 1) * P], selr[0:E, :], start=True, stop=True)
            mm.then_inc(a_picked, 1)
            pe.wait_ge(rpb_ready, 1)
            pe.wait_ge(ctx_left, 1)
            nc.tensor.matmul(Z[:, 0:EA], rpbc, selr[0:E, :], start=True, stop=True).then_inc(bias4_made, 1)
            pe.wait_ge(padded, 3)
            pe.wait_ge(t_lo, 1)
            pe.wait_ge(x_lo, 1)
            for mb in range(MB):
                conv(0, mb, mb + 1)
            pe.wait_ge(x_lo, 2)
            for mb in range(MB):
                conv(1, mb, MB + mb + 1)
            pe.wait_ge(b_rest, 2)
            pe.wait_ge(a_left, 2)
            for oc in range(NOC):
                if oc >= 2:
                    pe.wait_ge(b_left, 2 * (oc - 1))
                for bank, parts in ((Y[2 - 2 * (oc % 2)], (0, 1, 2, 0)), (Y[3 - 2 * (oc % 2)], (1, 0))):
                    for i, p in enumerate(parts):
                        mm = nc.tensor.matmul(bank[i * ZR:(i + 1) * ZR, :], selb[:, :], BP[p][:, oc * OC:(oc + 1) * OC],
                                              start=True, stop=True)
                mm.then_inc(b_picked, 1)

            pe.wait_ge(a_lo, 2)
            pe.wait_ge(b_left, 2 * NOC)
            pe.wait_ge(h_lo, 4)
            products(0, 0, FIRST_BANK[0, 0], fresh=True)
            pe.wait_ge(h_lo, 8)
            pe.wait_ge(bank_free, 2 * MB + START_C)
            products(1, 0, FIRST_BANK[1, 0], zbank=Z1)
            products(0, 1, FIRST_BANK[0, 1], fresh=True)
            turn(0, 0, 2)
            turn(1, 1, 2)
            products(1, 1, FIRST_BANK[1, 1])
            pe.wait_ge(zT_ready, 2)
            pe.wait_ge(b_scaled, 2)
            for t, oc in FIRST[0:4]:
                lora(t, oc, FIRST_BANK[t, oc])
            products(0, 2, FIRST_BANK[0, 2], fresh=True)
            pe.wait_ge(b_scaled, 3)
            lora(0, 2, FIRST_BANK[0, 2])
            pe.wait_ge(y_free, 2 + START_Y)
            products(1, 2, FIRST_BANK[1, 2])
            lora(1, 2, FIRST_BANK[1, 2])
            products(0, 3, FIRST_BANK[0, 3], fresh=True)
            pe.wait_ge(b_scaled, 4)
            lora(0, 3, FIRST_BANK[0, 3])
            pe.wait_ge(x_lo, 3)
            pe.wait_ge(y_free, 6 + START_Y)
            for mb in range(MB):
                conv(2, mb, 2 * MB + mb + 1)
            pe.wait_ge(y_free, 7 + START_Y)
            products(1, 3, FIRST_BANK[1, 3])
            lora(1, 3, FIRST_BANK[1, 3])

            def tile(t, b, more):
                def chunk(oc):
                    pe.wait_ge(y_free, 4 * t + oc + 1)
                    products(b, oc, Y[oc])

                pe.wait_ge(h_lo, 4 * (t + 1))
                chunk(0)
                if more:
                    pe.wait_ge(x_lo, t + 2)
                    conv(t + 1, 0, 4 * (t + 1) + 1)
                    conv(t + 1, 1, 4 * (t + 1) + 2)
                chunk(1)
                turn(t, b, t + 1)
                if more:
                    conv(t + 1, 2, 4 * (t + 1) + 3)
                    conv(t + 1, 3, 4 * (t + 1) + 4)
                pe.wait_ge(zT_ready, t + 1)
                lora(b, 0, Y[0])
                lora(b, 1, Y[1])
                chunk(2)
                lora(b, 2, Y[2])
                chunk(3)
                lora(b, 3, Y[3])

            with pe.Fori(2, N - 2, 2) as t:
                for b in range(2):
                    tile(t + b, b, True)
            tile(N - 2, 0, True)
            tile(N - 1, 1, False)


_OUT = (N, P, L)


def kernel(**inputs):
    import numpy as np
    import concourse.bacc as bacc
    from concourse.bass_utils import run_bass_kernel_spmd as run

    i = {k: np.asarray(v) for k, v in inputs.items()}
    arrays = {
        "xc": i["x"].reshape(N, G, CG, M, R).transpose(0, 4, 2, 1, 3).reshape(N, P, G, M),
        "xr": i["x"],
        "wconv": i["L0_cond_weight"].reshape(G, CG, CG, K)[:, :, :, ::-1].transpose(2, 0, 3, 1).reshape(CG, G, K * CG),
        "condT": i["cond_128"].T,
        "cwT": i["L0_cond_c_weight"].T,
        "bias": i["fside_S_0"].reshape(1, P),
        "wt": i["L0_ffn_W_base"].reshape(NOC, OC, MB, P, R).transpose(0, 3, 2, 4, 1).reshape(NOC, P, KB * OC),
        "loraA": i["L0_ffn_lora_A"].reshape(E * RK, MB, P, R).transpose(0, 1, 3, 2).reshape(E * RK, L),
        "routerW": i["L0_ffn_router_W"].reshape(E, MB, P, R).transpose(0, 1, 3, 2).reshape(E, L),
        "loraB": i["L0_ffn_lora_B"].transpose(0, 2, 1).reshape(E * RK, O),
        "b_base": i["L0_ffn_b_base"].reshape(P, O // P),
        "router_b": i["L0_ffn_router_b"].reshape(E, 1),
        "prior": i["L0_ffn_domain_prior"].reshape(E, 1),
        "active": i["L0_ffn_active"].reshape(1, EA),
    }
    arrays = {k: np.ascontiguousarray(v) for k, v in arrays.items()}
    nc = bacc.Bacc("TRN2", target_bir_lowering=False, num_devices=1, dynamic_dma_scratch_size=4096)
    args = [nc.dram_tensor(k, v.shape, mybir.dt.from_np(v.dtype), kind="ExternalInput").ap() for k, v in arrays.items()]
    args.append(nc.dram_tensor("out", _OUT, F32, kind="ExternalOutput").ap())
    adaln_ffn(nc, *args)
    return run(nc, [arrays], core_ids=[0]).results[0]["out"]
```

```python
from contextlib import ExitStack

import concourse.bass as bass
from concourse import mybir

ALU = mybir.AluOpType
ACT = mybir.ActivationFunctionType
AX = mybir.AxisListType
F32 = mybir.dt.float32
F16 = mybir.dt.float16
BF16 = mybir.dt.bfloat16
I32 = mybir.dt.int32
ABSMAX = bass.bass_isa.ReduceOp.absmax

P = 128
N = 32
L = 2048
O = 2048
G = 4
CG = 32
K = 9
R = 4
M = L // R
TAP = K + R - 1
OC = 512
NOC = O // OC
KB = L // P
MB = M // P
E = 16
EA = 4
RK = 8
ZR = EA * RK
ZC = ZR + EA
SCALING = 16.0 / 8.0
EPS = 1e-12
EXPONENT = 0x7F800000
TOP = 2.0 ** 13
UNTOP = 2.0 ** -14
FLOOR = 2.0 ** -40
LAG = 5
HUGE = 3e38
START_C = 2
START_Y = NOC
SM_STEPS = 14


def adaln_ffn(nc, xc, xr, wconv, ctx_w, bias, cw, wt, loraA, routerW, loraB, b_base, router_bp, active, out):
    ctx_rows = nc.dram_tensor("ctx_rows", (N, P), F32).ap()

    with ExitStack() as ctx:
        def sb(name, shape, dt):
            return ctx.enter_context(nc.sbuf_tensor(name, shape, dt))

        def sem(name):
            return ctx.enter_context(nc.semaphore(name))

        W16 = sb("W16", [P, (NOC * KB + LAG) * 2 * OC], F16)
        W32 = W16[:, :].bitcast(F32)
        xf = sb("xf", [P, G, M], F32)
        xh = sb("xh", [P, 2, G, M + 2], F16)
        hs = sb("hs", [P, 2, OC], F32)
        h16 = sb("h16", [P, 2, 2, KB, P], F16)
        T16 = sb("T16", [P, 2, G, TAP * CG], F16)
        A16 = sb("A16", [P, KB, 2 * ZC], F16)
        B16 = sb("B16", [3 * ZR, O], F16)
        biasb = sb("biasb", [P, O], F32)
        xres = sb("xres", [P, 2, O], F32)
        ctxb = sb("ctxb", [P, P], F32)
        ctxs = sb("ctxs", [P, P], F32)
        ident = sb("ident", [P, P], F16)
        zcat = sb("zcat", [P, 2, P], F16)
        zT = sb("zT", [P, 2, P], F16)
        sc = sb("sc", [P, 2, 8], F32)
        tmp = sb("tmp", [P, 8], F32)
        yinv = sb("yinv", [P, 2, 8], F32)
        cst = sb("cst", [P, 16], F32)
        cmx = sb("cmx", [P, 16], F32)
        wmx = sb("wmx", [P, NOC, KB], F32)
        junk = sb("junk", [P, 2, OC], BF16)
        wam = sb("wam", [P, NOC, 2], F32)
        wsc = sb("wsc", [P, NOC, 2], F32)
        amx = sb("amx", [P, 2], F32)
        zs = sb("zs", [P, 2 * ZC], F32)
        zr = sb("zr", [P, ZR], F32)
        sm = sb("sm", [P, 26], F32)
        sel = sb("sel", [P, 3 * ZR], F32)
        picks = sb("picks", [P, 2], F32)
        selr = sb("selr", [P, EA], F32)
        acti = sb("acti", [P, EA], I32)
        part = sb("part", [P, 1], I32)
        actf = sb("actf", [P, 4, EA], F32)
        jrow = sb("jrow", [P, EA], F32)
        pcol = sb("pcol", [P, 1], F32)
        rbp = sb("rbp", [P, 4], F32)
        bias4 = sb("bias4", [P, EA], F32)
        onesr = sb("onesr", [1, P], F32)
        biasr = sb("biasr", [1, P], F32)

        T32 = h16[:, 1, :, :, :].rearrange("p a k c -> p (a k c)").bitcast(F32)[:, 0:G * TAP * CG].rearrange("p (g c) -> p g c", g=G)
        early = h16[:, 0, :, :, :].rearrange("p a k c -> p (a k c)").bitcast(F32)
        cT_sb = early[:, 0:N]
        cwT_sb = early[:, N:N + P]
        ctxn = early[0:N, 2 * P:3 * P]
        iot = early[:, 3 * P:4 * P]
        ioti = early[:, 4 * P:5 * P].bitcast(I32)
        cw_sb = early[:, 5 * P:5 * P + CG * K]
        late = W32[:, ((NOC - 1) * KB + LAG) * OC:(NOC * KB + LAG) * OC]
        A_raw = late[:, 0:L]
        R_raw = late[0:E, L:2 * L]
        AT32 = late[:, 2 * L:2 * L + KB * ZC].rearrange("p (k c) -> p k c", k=KB)
        rpbc = late[0:E, 2 * L + KB * ZC:2 * L + KB * ZC + P]
        B_raw = xres[:, 1, :]

        Y = [ctx.enter_context(nc.psum_tensor(f"Y{i}", [P, OC], F32)) for i in range(NOC)]
        C = [ctx.enter_context(nc.psum_tensor(f"C{i}", [P, OC], F32)) for i in range(2)]
        Z = ctx.enter_context(nc.psum_tensor("Z", [P, OC], F32))
        Z1 = ctx.enter_context(nc.psum_tensor("Z1", [P, OC], F32))
        Q = Z1[:, :].bitcast(F16)

        in_act = sem("in_act")
        in_ctx = sem("in_ctx")
        in_T = sem("in_T")
        in_cw = sem("in_cw")
        in_A = sem("in_A")
        in_R = sem("in_R")
        in_B = sem("in_B")
        in_rb = sem("in_rb")
        in_b = sem("in_b")
        in_W = [[sem(f"in_W{i}_{q}") for q in range(4)] for i in range(NOC)]
        iotas = sem("iotas")
        padded = sem("padded")
        t_zeroed = sem("t_zeroed")
        dve_link = sem("dve_link")
        sel_ready = sem("sel_ready")
        prior_ready = sem("prior_ready")
        log_ready = sem("log_ready")
        rpb_ready = sem("rpb_ready")
        bias4_made = sem("bias4_made")
        bias4_left = sem("bias4_left")
        ctx_made = sem("ctx_made")
        ctx_left = sem("ctx_left")
        ctx_stored = sem("ctx_stored")
        c_max = sem("c_max")
        c_allmax = sem("c_allmax")
        c_scale = sem("c_scale")
        t_hi = sem("t_hi")
        t_lo = sem("t_lo")
        a_picked = sem("a_picked")
        a_left = sem("a_left")
        a_max = sem("a_max")
        a_allmax = sem("a_allmax")
        a_scale = sem("a_scale")
        a_hi = sem("a_hi")
        a_lo = sem("a_lo")
        b_picked = sem("b_picked")
        b_max = sem("b_max")
        b_allmax = sem("b_allmax")
        b_scale = sem("b_scale")
        b_hi = sem("b_hi")
        b_lo = sem("b_lo")
        w_sum = sem("w_sum")
        w_qmax = sem("w_qmax")
        w_max = sem("w_max")
        w_allmax = sem("w_allmax")
        w_scale = sem("w_scale")
        w_hi = sem("w_hi")
        w_lo = sem("w_lo")
        x_in = sem("x_in")
        c_in = sem("c_in")
        xr_in = [sem("xr_in0"), sem("xr_in1")]
        x_max = sem("x_max")
        x_allmax = sem("x_allmax")
        max_seen = sem("max_seen")
        scale_step = sem("scale_step")
        x_scale = sem("x_scale")
        ctx_scaled = sem("ctx_scaled")
        x_hi = sem("x_hi")
        x_lo = sem("x_lo")
        conv_done = sem("conv_done")
        bank_free = sem("bank_free")
        h_hi = sem("h_hi")
        h_lo = sem("h_lo")
        z_done = sem("z_done")
        l_undo = sem("l_undo")
        first_undo = sem("first_undo")
        sm_step = sem("sm_step")
        sm_exp = sem("sm_exp")
        z_ready = sem("z_ready")
        z_turned = sem("z_turned")
        zT_ready = sem("zT_ready")
        y_done = sem("y_done")
        l_done = sem("l_done")
        l_free = sem("l_free")
        biased = sem("biased")
        y_free = sem("y_free")
        out_done = sem("out_done")

        block = ctx.enter_context(nc.Block())

        FIRST = [(0, 0), (1, 0), (0, 1), (1, 1), (0, 2), (1, 2), (0, 3), (1, 3)]
        L_FIRST = [C[0], C[1], Z, C[0], C[1], Z, Y[0], Y[1]]
        L_BANK = [C[0], C[1], C[0], Z]
        MAX_QUARTERS = [2, 1, 1, 1]
        B_BANK = [Y[1], Z1, Y[2], Y[3]]

        def wslot(oc, kb, half):
            at = ((oc * KB + kb) * 2 + half) * OC
            return W16[:, at:at + OC]

        def wraw(oc, kb, n=1):
            at = (oc * KB + kb + LAG) * OC
            return W32[:, at:at + n * OC]

        @block.sync
        def _(sp):
            def load_ctx(n):
                row = ctx_rows[n:n + 1, :] if isinstance(n, int) else ctx_rows[bass.ds(n, 1), :]
                sp.dma_start(ctxb[:, :], row.partition_broadcast(P)).then_inc(c_in, 16)

            def load_x(n):
                sp.wait_ge(x_hi, n)
                sp.wait_ge(x_lo, n)
                sp.dma_start(xf[:, :, :], xc[n]).then_inc(x_in, 16)
                load_ctx(n)

            def load_res(n, b):
                sp.dma_start(xres[:, b, :], xr[n]).then_inc(xr_in[b], 16)

            def load_w(oc):
                for q in range(4):
                    sp.dma_start(wraw(oc, 4 * q, 4), wt[oc, :, q * 4 * OC:(q + 1) * 4 * OC]).then_inc(in_W[oc][q], 16)

            sp.dma_start(cw_sb, cw).then_inc(in_cw, 16)
            sp.dma_start(xf[:, :, :], xc[0]).then_inc(x_in, 16)
            sp.wait_ge(t_zeroed, 1)
            for r in range(R):
                sp.dma_start(T32[r * CG:(r + 1) * CG, :, r * CG:(r + K) * CG], wconv).then_inc(in_T, 16)
            sp.dma_start(A_raw, loraA).then_inc(in_A, 16)
            sp.dma_start(R_raw, routerW).then_inc(in_R, 16)
            sp.dma_start(rbp[0:E, 0:2], router_bp).then_inc(in_rb, 16)
            sp.wait_ge(ctx_stored, 16)
            load_ctx(0)
            load_w(0)
            load_x(1)
            sp.dma_start(B_raw, loraB).then_inc(in_B, 16)
            sp.dma_start(biasb[:, :], b_base.partition_broadcast(P)).then_inc(in_b, 16)
            load_w(1)
            load_w(2)
            load_res(0, 0)
            sp.wait_ge(b_picked, NOC)
            sp.wait_ge(b_max, 1)
            load_res(1, 1)
            load_x(2)
            sp.wait_ge(a_lo, 2)
            load_w(3)
            load_x(3)
            for t in range(2):
                sp.wait_ge(y_free, START_Y + 7 + t)
                sp.wait_ge(l_free, NOC * (t + 1))
                sp.wait_ge(biased, t + 1)
                for oc in range(NOC):
                    sp.dma_start(out[t, :, oc * OC:(oc + 1) * OC], xres[:, t, oc * OC:(oc + 1) * OC]).then_inc(out_done, 16)
                sp.wait_ge(out_done, 64 * (t + 1))
                load_res(t + 2, t)
            load_x(4)

            def store(t, b, oc):
                if oc < NOC - 1:
                    sp.wait_ge(l_free, 4 * t + oc + 1)
                else:
                    sp.wait_ge(y_free, 4 * t + oc + 1 + START_Y)
                sp.dma_start(out[t, :, oc * OC:(oc + 1) * OC], xres[:, b, oc * OC:(oc + 1) * OC]).then_inc(out_done, 16)

            def tile(t, b, more_x, more_res):
                store(t, b, 0)
                store(t, b, 1)
                if more_x:
                    load_x(t + 3)
                store(t, b, 2)
                store(t, b, 3)
                if more_res:
                    sp.wait_ge(out_done, 64 * (t + 1))
                    load_res(t + 2, b)

            with sp.Fori(2, N - 4, 2) as t:
                for b in range(2):
                    tile(t + b, b, True, True)
            tile(N - 4, 0, True, True)
            for t in range(N - 3, N):
                tile(t, t % 2, False, t < N - 2)
            sp.wait_ge(out_done, 64 * N)

        @block.gpsimd
        def _(pool):
            nc.gpsimd.memset(T32, 0.0).then_inc(t_zeroed, 1)
            nc.gpsimd.iota(ioti, [[1, P]], base=0, channel_multiplier=0).then_inc(iotas, 1)
            nc.gpsimd.iota(part[:, :], [[0, 1]], base=0, channel_multiplier=1).then_inc(iotas, 1)
            nc.gpsimd.memset(onesr[:, :], 1.0).then_inc(padded, 1)
            nc.gpsimd.memset(xh[:, :, :, 0:1], 0.0).then_inc(padded, 1)
            nc.gpsimd.memset(xh[:, :, :, M + 1:M + 2], 0.0).then_inc(padded, 1)
            nc.gpsimd.memset(zcat[:, :, :], 0.0).then_inc(padded, 1)
            pool.wait_ge(padded, 4)

            def all_max(oc):
                pool.wait_ge(w_max, oc + 1)
                nc.gpsimd.partition_all_reduce(wam[:, oc, 1:2], wam[:, oc, 0:1], P, ABSMAX).then_inc(w_allmax, 1)
                pool.wait_ge(w_allmax, oc + 1)

            pool.wait_ge(c_max, 1)
            nc.gpsimd.partition_all_reduce(cmx[:, 8:11], cmx[:, 0:3], P, ABSMAX).then_inc(c_allmax, 1)
            pool.wait_ge(c_allmax, 1)
            pool.wait_ge(x_max, 1)
            nc.gpsimd.partition_all_reduce(amx[:, 1:2], amx[:, 0:1], P, ABSMAX).then_inc(x_allmax, 1)
            pool.wait_ge(x_allmax, 1)
            all_max(0)
            pool.wait_ge(x_max, 2)
            nc.gpsimd.partition_all_reduce(amx[:, 1:2], amx[:, 0:1], P, ABSMAX).then_inc(x_allmax, 1)
            pool.wait_ge(x_allmax, 2)
            pool.wait_ge(a_max, 1)
            nc.gpsimd.partition_all_reduce(cmx[:, 11:13], cmx[:, 3:5], P, ABSMAX).then_inc(a_allmax, 1)
            pool.wait_ge(a_allmax, 1)
            pool.wait_ge(b_max, 1)
            nc.gpsimd.partition_all_reduce(cmx[:, 13:14], cmx[:, 5:6], P, ABSMAX).then_inc(b_allmax, 1)
            pool.wait_ge(b_allmax, 1)
            for oc in range(1, NOC):
                all_max(oc)

            with pool.Fori(2, N, 1) as n:
                pool.wait_ge(x_max, n + 1)
                pool.sem_inc(max_seen, 1)
                nc.gpsimd.partition_all_reduce(amx[:, 1:2], amx[:, 0:1], P, ABSMAX).then_inc(x_allmax, 1)

        @block.scalar
        def _(act):
            act.dma_start(acti[:, :], active.partition_broadcast(P)).then_inc(in_act, 16)
            act.dma_start(early[:, 0:N + P], ctx_w).then_inc(in_ctx, 16)
            act.dma_start(biasr[:, :], bias).then_inc(in_ctx, 16)
            act.wait_ge(ctx_made, 1)
            nc.scalar.copy(ctxn, Z[0:N, 0:P]).then_inc(ctx_left, 1)
            act.wait_ge(ctx_left, 1)
            act.dma_start(ctx_rows, ctxn).then_inc(ctx_stored, 16)

            def split_x(n, b):
                act.wait_ge(x_scale, n + 1)
                nc.scalar.activation(xh[:, 0, :, 1:M + 1], xf[:, :, :], ACT.Copy, scale=sc[:, b, 1:2]).then_inc(x_hi, 1)

            def split_h(n, b, mb):
                act.wait_ge(bank_free, 4 * n + mb + 1 + START_C)
                nc.scalar.activation(h16[:, b, 0, 4 * mb:4 * mb + 4, :].rearrange("p k c -> p (k c)"), hs[:, mb % 2, :],
                                     ACT.Copy, scale=sc[:, b, 2:3]).then_inc(h_hi, 1)

            def split_w(oc, kbs):
                act.wait_ge(w_scale, oc + 1)
                for kb in kbs:
                    if oc * KB + kb >= LAG:
                        act.wait_ge(w_lo, oc * KB + kb - LAG + 1)
                    nc.scalar.activation(wslot(oc, kb, 0), wraw(oc, kb), ACT.Copy, scale=wsc[:, oc, 0:1]).then_inc(w_hi, 1)

            summed = [0]

            def sum_w(oc, qs):
                for q in qs:
                    act.wait_ge(in_W[oc][q], 16)
                    for kb in range(4 * q, 4 * q + 4):
                        summed[0] += 1
                        if summed[0] > 2:
                            act.wait_ge(w_sum, summed[0] - 2)
                        nc.scalar.activation(junk[:, summed[0] % 2, :], wraw(oc, kb), ACT.Abs,
                                             accum_out=wmx[:, oc, kb:kb + 1]).then_inc(w_sum, 1)

            def exp(t):
                act.wait_ge(sm_step, SM_STEPS * t + 4)
                nc.scalar.activation(sm[:, 8:12], sm[:, 0:4], ACT.Exp, bias=sm[:, 4:5], accum_out=sm[:, 12:13]).then_inc(sm_exp, 1)

            def copy_zT(t, b, turned):
                act.wait_ge(z_turned, turned)
                nc.scalar.copy(zT[:, b, :], Q[:, b * P:(b + 1) * P]).then_inc(zT_ready, 1)

            act.wait_ge(c_scale, 1)
            act.wait_ge(in_T, 16 * R)
            nc.scalar.activation(T16[:, 0, :, :], T32, ACT.Copy, scale=cst[:, 0:1]).then_inc(t_hi, 1)
            split_x(0, 0)
            act.wait_ge(prior_ready, 1)
            nc.scalar.activation(rbp[0:E, 2:3], rbp[0:E, 1:2], ACT.Ln).then_inc(log_ready, 1)
            act.wait_ge(ctx_stored, 16)
            split_h(0, 0, 0)
            split_h(0, 0, 1)
            sum_w(0, range(MAX_QUARTERS[0], 4))
            split_h(0, 0, 2)
            split_h(0, 0, 3)
            split_w(0, range(KB))
            split_x(1, 1)
            act.wait_ge(a_picked, 3)
            for i in range(2):
                nc.scalar.copy(AT32[:, i * KB // 2:(i + 1) * KB // 2, :],
                               Y[i + 1][:, 0:KB // 2 * ZC].rearrange("p (k c) -> p k c", c=ZC)).then_inc(a_left, 1)
            sum_w(1, range(MAX_QUARTERS[1], 3))
            act.wait_ge(a_scale, 1)
            nc.scalar.activation(A16[:, :, 0:ZR], AT32[:, :, 0:ZR], ACT.Copy, scale=cst[:, 3:4]).then_inc(a_hi, 1)
            nc.scalar.activation(A16[:, :, ZR:ZC], AT32[:, :, ZR:ZC], ACT.Copy, scale=cst[:, 4:5]).then_inc(a_hi, 1)
            act.wait_ge(t_lo, 1)
            split_h(1, 1, 0)
            split_h(1, 1, 1)
            split_h(1, 1, 2)
            split_h(1, 1, 3)
            act.wait_ge(b_picked, NOC)
            act.wait_ge(b_scale, 1)
            for oc in range(NOC):
                nc.scalar.activation(B16[:, oc * OC:(oc + 1) * OC], B_BANK[oc][0:3 * ZR, :], ACT.Copy,
                                     scale=cst[0:3 * ZR, 5:6]).then_inc(b_hi, 1)
            sum_w(1, [3])
            exp(0)
            split_w(1, range(KB))
            sum_w(2, range(MAX_QUARTERS[2], 3))
            exp(1)
            sum_w(2, [3])
            split_w(2, range(KB))
            sum_w(3, range(MAX_QUARTERS[3], 3))
            copy_zT(0, 0, 2)
            copy_zT(1, 1, 2)
            sum_w(3, [3])
            split_w(3, range(3 * KB // 4))
            split_x(2, 0)
            split_w(3, range(3 * KB // 4, KB))
            for mb in range(MB):
                split_h(2, 0, mb)
            split_x(3, 1)

            def tile(t, b, conv, split):
                exp(t)
                if conv:
                    split_h(t + 1, 1 - b, 0)
                    split_h(t + 1, 1 - b, 1)
                copy_zT(t, b, t + 1)
                if conv:
                    split_h(t + 1, 1 - b, 2)
                    split_h(t + 1, 1 - b, 3)
                if split:
                    split_x(t + 2, b)

            with act.Fori(2, N - 2, 2) as t:
                for b in range(2):
                    tile(t + b, b, True, True)
            tile(N - 2, 0, True, False)
            tile(N - 1, 1, False, False)

        @block.vector
        def _(dve):
            step = [0]

            def link(ins):
                step[0] += 1
                ins.then_inc(dve_link, 1)
                dve.wait_ge(dve_link, step[0])

            nc.vector.memset(cmx[:, :], FLOOR).then_inc(y_free, START_Y)
            nc.vector.memset(tmp[:, :], 0.0).then_inc(bank_free, START_C)
            dve.wait_ge(in_act, 16)
            link(nc.vector.tensor_copy(actf[:, 0, :], acti[:, :]))
            link(nc.vector.tensor_scalar(actf[:, 1, :], actf[:, 0, :], 0.0, float(E), ALU.is_lt, ALU.mult))
            link(nc.vector.tensor_tensor(actf[:, 2, :], actf[:, 0, :], actf[:, 1, :], ALU.add))
            link(nc.vector.tensor_scalar(actf[:, 3, :], actf[:, 2, :], 0.0, float(E - 1), ALU.max, ALU.min))
            dve.wait_ge(iotas, 2)
            link(nc.vector.tensor_scalar(jrow[:, :], actf[:, 3, :], float(RK), None, ALU.mult))
            nc.vector.tensor_copy(iot, ioti)
            link(nc.vector.tensor_copy(pcol[:, :], part[:, :]))
            for j in range(EA):
                ins = nc.vector.tensor_scalar(sel[:, RK * j:RK * j + RK], iot[:, 0:RK], jrow[:, j:j + 1], None, ALU.add)
            link(ins)
            link(nc.vector.tensor_scalar(sel[:, 0:ZR], sel[:, 0:ZR], pcol[:, 0:1], None, ALU.is_equal))
            nc.vector.tensor_copy(sel[:, ZR:3 * ZR].rearrange("p (n c) -> p n c", n=2),
                                  sel[:, 0:ZR].rearrange("p (o c) -> p o c", o=1).to_broadcast([P, 2, ZR]))
            nc.vector.tensor_reduce(picks[:, 0:1], sel[:, 0:ZR], AX.X, ALU.max)
            nc.vector.tensor_scalar(ident[:, :], iot, pcol[:, 0:1], None, ALU.is_equal)
            nc.vector.tensor_scalar(selr[:, :], actf[:, 3, :], pcol[:, 0:1], None, ALU.is_equal).then_inc(sel_ready, 1)

            def max_x(n):
                dve.wait_ge(x_in, 16 * (n + 1))
                nc.vector.tensor_reduce(amx[:, 0:1], xf[:, :, :], AX.XY, ALU.max, apply_absolute_value=True).then_inc(x_max, 1)

            SCALE_STEPS = 5

            def scale_x(n, b):
                def wait(k):
                    dve.wait_ge(scale_step, SCALE_STEPS * n + k)

                if not (isinstance(n, int) and n == 0):
                    dve.wait_ge(h_lo, 4 * n)
                dve.wait_ge(x_allmax, n + 1)
                nc.vector.tensor_scalar(sc[:, b, 0:1], amx[:, 1:2], FLOOR, None, ALU.max).then_inc(scale_step, 1)
                wait(1)
                nc.vector.tensor_scalar(tmp[:, 0:1].bitcast(I32), sc[:, b, 0:1].bitcast(I32), EXPONENT, EXPONENT,
                                        ALU.bitwise_and, ALU.bitwise_xor)
                nc.vector.tensor_scalar(tmp[:, 1:2].bitcast(I32), sc[:, b, 0:1].bitcast(I32), EXPONENT, None, ALU.bitwise_and)
                nc.vector.tensor_scalar(tmp[:, 2:3], sc[:, b, 0:1], cmx[:, 10:11], cmx[:, 9:10], ALU.mult, ALU.add).then_inc(scale_step, 1)
                wait(2)
                nc.vector.tensor_scalar(tmp[:, 3:4].bitcast(I32), tmp[:, 2:3].bitcast(I32), EXPONENT, EXPONENT,
                                        ALU.bitwise_and, ALU.bitwise_xor)
                nc.vector.tensor_scalar(sc[:, b, 4:5].bitcast(I32), tmp[:, 2:3].bitcast(I32), EXPONENT, None, ALU.bitwise_and)
                nc.vector.tensor_scalar(sc[:, b, 1:2], tmp[:, 0:1], TOP, None, ALU.mult)
                nc.vector.tensor_scalar(tmp[:, 4:5], tmp[:, 1:2], UNTOP, cst[:, 8:9], ALU.mult, ALU.mult).then_inc(scale_step, 1)
                wait(3)
                nc.vector.tensor_scalar(sc[:, b, 3:4], tmp[:, 3:4], TOP, None, ALU.mult).then_inc(scale_step, 1)
                nc.vector.tensor_scalar(tmp[:, 5:6], sc[:, b, 1:2], cst[:, 0:1], None, ALU.mult).then_inc(scale_step, 1)
                wait(5)
                nc.vector.tensor_tensor(sc[:, b, 2:3], tmp[:, 4:5], sc[:, b, 3:4], ALU.mult).then_inc(x_scale, 1)

            def split_x(n, b):
                dve.wait_ge(x_hi, n + 1)
                nc.vector.scalar_tensor_tensor(out=xh[:, 1, :, 1:M + 1], in0=xf[:, :, :], scalar=sc[:, b, 1:2],
                                               in1=xh[:, 0, :, 1:M + 1], op0=ALU.mult, op1=ALU.subtract).then_inc(x_lo, 1)

            def scale_ctx(n):
                dve.wait_ge(c_in, 16 * (n + 1))
                nc.vector.tensor_scalar(ctxs[:, :], ctxb[:, :], tmp[:, 5:6], None, ALU.mult).then_inc(ctx_scaled, 1)

            def stage_h(n, mb):
                if mb >= 2 or not (isinstance(n, int) and n == 0):
                    dve.wait_ge(h_lo, 4 * n + mb - 1)
                if mb == 0:
                    dve.wait_ge(ctx_scaled, n + 1)
                dve.wait_ge(conv_done, 4 * n + mb + 1)
                nc.vector.tensor_tensor(hs[:, mb % 2, :].rearrange("p (r g c) -> p r g c", r=R, g=G),
                                        C[mb % 2][:, :].rearrange("p (g r c) -> p r g c", r=R, g=G),
                                        ctxs[:, :].rearrange("p (o g c) -> p o g c", o=1, g=G).to_broadcast([P, R, G, CG]),
                                        ALU.add).then_inc(bank_free, 1)

            def split_h(n, b, mb):
                dve.wait_ge(h_hi, 4 * n + mb + 1)
                nc.vector.scalar_tensor_tensor(out=h16[:, b, 1, 4 * mb:4 * mb + 4, :].rearrange("p k c -> p (k c)"), in0=hs[:, mb % 2, :],
                                               scalar=sc[:, b, 2:3], in1=h16[:, b, 0, 4 * mb:4 * mb + 4, :].rearrange("p k c -> p (k c)"),
                                               op0=ALU.mult, op1=ALU.subtract).then_inc(h_lo, 1)

            def conv_half(n, b, half):
                for mb in (2 * half, 2 * half + 1):
                    stage_h(n, mb)
                for mb in (2 * half, 2 * half + 1):
                    split_h(n, b, mb)

            def make_scales(lo, hi):
                link(nc.vector.tensor_scalar(cmx[:, 8 + lo:8 + hi], cmx[:, 8 + lo:8 + hi], FLOOR, None, ALU.max))
                nc.vector.tensor_scalar(cst[:, lo:hi].bitcast(I32), cmx[:, 8 + lo:8 + hi].bitcast(I32), EXPONENT, EXPONENT,
                                        ALU.bitwise_and, ALU.bitwise_xor)
                link(nc.vector.tensor_scalar(cst[:, 8 + lo:8 + hi].bitcast(I32), cmx[:, 8 + lo:8 + hi].bitcast(I32), EXPONENT, None,
                                             ALU.bitwise_and))
                nc.vector.tensor_scalar(cst[:, 8 + lo:8 + hi], cst[:, 8 + lo:8 + hi], UNTOP, None, ALU.mult)
                return nc.vector.tensor_scalar(cst[:, lo:hi], cst[:, lo:hi], TOP, None, ALU.mult)

            def max_w(oc, qs):
                for q in qs:
                    dve.wait_ge(in_W[oc][q], 16)
                    nc.vector.tensor_reduce(wmx[:, oc, 4 * q:4 * q + 4], wraw(oc, 4 * q, 4).rearrange("p (k o) -> p k o", k=4), AX.X,
                                            ALU.max, apply_absolute_value=True).then_inc(w_qmax, 1)

            def scale_w(oc):
                maxed = sum(MAX_QUARTERS[0:oc + 1])
                dve.wait_ge(w_qmax, maxed)
                dve.wait_ge(w_sum, KB // 4 * (4 * (oc + 1) - maxed))
                nc.vector.tensor_reduce(wam[:, oc, 0:1], wmx[:, oc, :], AX.X, ALU.max).then_inc(w_max, 1)
                dve.wait_ge(w_allmax, oc + 1)
                link(nc.vector.tensor_scalar(wam[:, oc, 1:2], wam[:, oc, 1:2], FLOOR, None, ALU.max))
                nc.vector.tensor_scalar(wsc[:, oc, 0:1].bitcast(I32), wam[:, oc, 1:2].bitcast(I32), EXPONENT, EXPONENT,
                                        ALU.bitwise_and, ALU.bitwise_xor)
                link(nc.vector.tensor_scalar(wsc[:, oc, 1:2].bitcast(I32), wam[:, oc, 1:2].bitcast(I32), EXPONENT, None,
                                             ALU.bitwise_and))
                nc.vector.tensor_scalar(wsc[:, oc, 1:2], wsc[:, oc, 1:2], UNTOP, UNTOP, ALU.mult, ALU.mult)
                nc.vector.tensor_scalar(wsc[:, oc, 0:1], wsc[:, oc, 0:1], TOP, None, ALU.mult).then_inc(w_scale, 1)

            def low_w(oc, kbs):
                dve.wait_ge(w_scale, oc + 1)
                for kb in kbs:
                    dve.wait_ge(w_hi, oc * KB + kb + 1)
                    nc.vector.scalar_tensor_tensor(out=wslot(oc, kb, 1), in0=wraw(oc, kb), scalar=wsc[:, oc, 0:1],
                                                   in1=wslot(oc, kb, 0), op0=ALU.mult, op1=ALU.subtract).then_inc(w_lo, 1)

            dve.wait_ge(in_cw, 16)
            nc.vector.tensor_reduce(cmx[:, 0:1], cw_sb, AX.X, ALU.max, apply_absolute_value=True)
            nc.vector.tensor_reduce(cmx[:, 2:3], cw_sb, AX.X, ALU.add, apply_absolute_value=True)
            max_x(0)
            dve.wait_ge(ctx_left, 1)
            nc.vector.tensor_reduce(cmx[0:N, 1:2], ctxn, AX.X, ALU.max, apply_absolute_value=True).then_inc(c_max, 1)
            dve.wait_ge(c_allmax, 1)
            make_scales(0, 3).then_inc(c_scale, 1)
            dve.wait_ge(c_scale, 1)
            scale_x(0, 0)
            dve.wait_ge(in_rb, 16)
            nc.vector.tensor_scalar(rbp[0:E, 1:2], rbp[0:E, 1:2], EPS, None, ALU.add).then_inc(prior_ready, 1)
            dve.wait_ge(t_hi, 1)
            nc.vector.scalar_tensor_tensor(out=T16[:, 1, :, :], in0=T32, scalar=cst[:, 0:1],
                                           in1=T16[:, 0, :, :], op0=ALU.mult, op1=ALU.subtract).then_inc(t_lo, 1)
            scale_ctx(0)
            split_x(0, 0)
            dve.wait_ge(log_ready, 1)
            link(nc.vector.tensor_tensor(rbp[0:E, 3:4], rbp[0:E, 2:3], rbp[0:E, 0:1], ALU.add))
            link(nc.vector.memset(rpbc, 0.0))
            nc.vector.tensor_scalar(rpbc, rpbc, rbp[0:E, 3:4], None, ALU.add).then_inc(rpb_ready, 1)
            max_w(0, range(MAX_QUARTERS[0]))
            conv_half(0, 0, 0)
            stage_h(0, 2)
            stage_h(0, 3)
            scale_w(0)
            split_h(0, 0, 2)
            split_h(0, 0, 3)
            low_w(0, range(KB // 2))
            max_x(1)
            low_w(0, range(KB // 2, 3 * KB // 4))
            scale_x(1, 1)
            scale_ctx(1)
            low_w(0, range(3 * KB // 4, KB))
            split_x(1, 1)
            dve.wait_ge(a_left, 2)
            nc.vector.tensor_reduce(cmx[:, 3:4], AT32[:, :, 0:ZR], AX.XY, ALU.max, apply_absolute_value=True)
            nc.vector.tensor_reduce(cmx[:, 4:5], AT32[:, :, ZR:ZC], AX.XY, ALU.max, apply_absolute_value=True).then_inc(a_max, 1)
            dve.wait_ge(in_B, 16)
            link(nc.vector.tensor_reduce(picks[:, 1:2], B_raw, AX.X, ALU.max, apply_absolute_value=True))
            nc.vector.tensor_scalar(cmx[:, 5:6], picks[:, 1:2], HUGE, picks[:, 0:1], ALU.min, ALU.mult).then_inc(b_max, 1)
            dve.wait_ge(a_allmax, 1)
            make_scales(3, 5).then_inc(a_scale, 1)
            stage_h(1, 0)
            stage_h(1, 1)
            dve.wait_ge(b_allmax, 1)
            make_scales(5, 6).then_inc(b_scale, 1)
            dve.wait_ge(bias4_made, 1)
            nc.vector.tensor_copy(bias4[:, :], Z[:, 0:EA]).then_inc(bias4_left, 1)
            split_h(1, 1, 0)
            stage_h(1, 2)
            split_h(1, 1, 1)
            dve.wait_ge(a_hi, 2)
            nc.vector.scalar_tensor_tensor(out=A16[:, :, ZC:ZC + ZR], in0=AT32[:, :, 0:ZR], scalar=cst[:, 3:4],
                                           in1=A16[:, :, 0:ZR], op0=ALU.mult, op1=ALU.subtract).then_inc(a_lo, 1)
            nc.vector.scalar_tensor_tensor(out=A16[:, :, ZC + ZR:2 * ZC], in0=AT32[:, :, ZR:ZC], scalar=cst[:, 4:5],
                                           in1=A16[:, :, ZR:ZC], op0=ALU.mult, op1=ALU.subtract).then_inc(a_lo, 1)
            stage_h(1, 3)
            split_h(1, 1, 2)
            split_h(1, 1, 3)
            for oc in range(NOC):
                o = slice(oc * OC, (oc + 1) * OC)
                dve.wait_ge(b_hi, oc + 1)
                nc.vector.scalar_tensor_tensor(out=B16[ZR:2 * ZR, o], in0=B_BANK[oc][ZR:2 * ZR, :], scalar=cst[ZR:2 * ZR, 5:6],
                                               in1=B16[ZR:2 * ZR, o], op0=ALU.mult, op1=ALU.subtract).then_inc(b_lo, 1)
            max_w(1, range(MAX_QUARTERS[1]))
            scale_w(1)

            def softmax(t, b, bank=Z):
                def wait(k):
                    dve.wait_ge(sm_step, SM_STEPS * t + k)

                if not (isinstance(t, int) and t == 0):
                    dve.wait_ge(z_ready, t)
                dve.wait_ge(z_done, t + 1)
                nc.vector.tensor_scalar(yinv[:, b, 4:5], sc[:, b, 4:5], cst[:, 12:13], UNTOP, ALU.mult, ALU.mult)
                zb = bank[:, 0:2 * ZC]
                nc.vector.tensor_copy(zs[:, ZC:2 * ZC], zb[:, ZC:2 * ZC]).then_inc(sm_step, 1)
                wait(1)
                nc.vector.tensor_tensor(zs[:, 0:ZC], zb[:, 0:ZC], zs[:, ZC:2 * ZC], ALU.add).then_inc(sm_step, 1)
                wait(2)
                nc.vector.scalar_tensor_tensor(out=sm[:, 0:4], in0=zs[:, ZR:ZC], scalar=yinv[:, b, 4:5], in1=bias4[:, :],
                                               op0=ALU.mult, op1=ALU.add).then_inc(sm_step, 1)
                wait(3)
                nc.vector.tensor_reduce(sm[:, 4:5], sm[:, 0:4], AX.X, ALU.max, negate=True).then_inc(sm_step, 1)
                dve.wait_ge(sm_exp, t + 1)
                nc.vector.reciprocal(sm[:, 13:14], sm[:, 12:13]).then_inc(sm_step, 1)
                wait(5)
                nc.vector.tensor_scalar(sm[:, 16:20], sm[:, 8:12], sm[:, 13:14], cst[:, 11:12], ALU.mult, ALU.mult).then_inc(sm_step, 1)
                wait(6)
                nc.vector.tensor_tensor(zr[:, :].rearrange("p (j r) -> p j r", j=EA), zs[:, 0:ZR].rearrange("p (j r) -> p j r", j=EA),
                                        sm[:, 16:20].rearrange("p (j o) -> p j o", o=1).to_broadcast([P, EA, RK]), ALU.mult).then_inc(sm_step, 1)
                wait(7)
                nc.vector.tensor_reduce(sm[:, 20:21], zr[:, :], AX.X, ALU.max, apply_absolute_value=True).then_inc(sm_step, 1)
                wait(8)
                nc.vector.tensor_scalar(sm[:, 21:22], sm[:, 20:21], FLOOR, None, ALU.max).then_inc(sm_step, 1)
                wait(9)
                nc.vector.tensor_scalar(sm[:, 22:23].bitcast(I32), sm[:, 21:22].bitcast(I32), EXPONENT, EXPONENT,
                                        ALU.bitwise_and, ALU.bitwise_xor).then_inc(sm_step, 1)
                nc.vector.tensor_scalar(sm[:, 23:24].bitcast(I32), sm[:, 21:22].bitcast(I32), EXPONENT, None, ALU.bitwise_and).then_inc(sm_step, 1)
                wait(10)
                nc.vector.tensor_scalar(sm[:, 24:25], sm[:, 22:23], TOP, None, ALU.mult).then_inc(sm_step, 1)
                wait(11)
                nc.vector.tensor_scalar(sm[:, 25:26], sm[:, 23:24], UNTOP, cst[:, 13:14], ALU.mult, ALU.mult).then_inc(sm_step, 1)
                wait(12)
                nc.vector.tensor_scalar(zcat[:, b, 0:2 * ZR].rearrange("p (n c) -> p n c", n=2),
                                        zr[:, :].rearrange("p (o c) -> p o c", o=1).to_broadcast([P, 2, ZR]), sm[:, 24:25], None,
                                        ALU.mult).then_inc(sm_step, 1)
                wait(14)
                nc.vector.tensor_scalar(yinv[:, b, 5:6], sm[:, 25:26], sc[:, b, 4:5], UNTOP * SCALING, ALU.mult, ALU.mult).then_inc(l_undo, 1)
                nc.vector.scalar_tensor_tensor(out=zcat[:, b, 2 * ZR:3 * ZR], in0=zr[:, :], scalar=sm[:, 24:25],
                                               in1=zcat[:, b, 0:ZR], op0=ALU.mult, op1=ALU.subtract).then_inc(z_ready, 1)

            def leave(t, b, oc, bank, done):
                dve.wait_ge(y_done, done)
                nc.vector.scalar_tensor_tensor(out=xres[:, b, oc * OC:(oc + 1) * OC], in0=bank[:, :], scalar=yinv[:, b, oc:oc + 1],
                                               in1=xres[:, b, oc * OC:(oc + 1) * OC], op0=ALU.mult, op1=ALU.add).then_inc(y_free, 1)

            def add_lora(t, b, oc, bank):
                dve.wait_ge(l_done, 4 * t + oc + 1)
                nc.vector.scalar_tensor_tensor(out=xres[:, b, oc * OC:(oc + 1) * OC], in0=bank[:, :], scalar=yinv[:, b, 5:6],
                                               in1=xres[:, b, oc * OC:(oc + 1) * OC], op0=ALU.mult, op1=ALU.add).then_inc(l_free, 1)

            def add_bias(b):
                nc.vector.tensor_tensor(xres[:, b, :], xres[:, b, :], biasb[:, :], ALU.add).then_inc(biased, 1)

            def first_undo_scales(oc):
                dve.wait_ge(w_scale, oc + 1)
                for t in range(2):
                    nc.vector.tensor_scalar(yinv[:, t, oc:oc + 1], wsc[:, oc, 1:2], sc[:, t, 4:5], None, ALU.mult).then_inc(first_undo, 1)

            def leave_first(i):
                t, oc = FIRST[i]
                dve.wait_ge(first_undo, 2 * (oc + 1))
                leave(t, t, oc, Y[i % NOC], i + 1)

            def add_lora_first(k):
                add_lora(k // NOC, k // NOC, k % NOC, L_FIRST[k])

            dve.wait_ge(padded, 4)
            softmax(0, 0)
            low_w(1, range(KB))
            max_w(2, range(MAX_QUARTERS[2]))
            softmax(1, 1, Z1)
            scale_w(2)
            for oc in range(3):
                first_undo_scales(oc)
            dve.wait_ge(xr_in[0], 16)
            dve.wait_ge(xr_in[1], 16)
            leave_first(0)
            leave_first(1)
            low_w(2, range(KB))
            leave_first(2)
            max_w(3, range(MAX_QUARTERS[3]))
            leave_first(3)
            max_x(2)
            scale_w(3)
            first_undo_scales(3)
            dve.wait_ge(first_undo, 2 * NOC)
            scale_x(2, 0)
            scale_ctx(2)
            low_w(3, range(KB // 3))
            leave_first(4)
            dve.wait_ge(y_free, START_Y + 3)
            add_lora_first(0)
            add_lora_first(1)
            dve.wait_ge(y_free, START_Y + 5)
            add_lora_first(2)
            low_w(3, range(KB // 3, KB))
            leave_first(5)
            for k in (3, 4):
                add_lora_first(k)
            split_x(2, 0)
            add_lora_first(5)
            dve.wait_ge(l_free, 4)
            leave_first(6)
            dve.wait_ge(y_free, START_Y + 6)
            add_lora_first(6)
            add_lora_first(7)
            conv_half(2, 0, 0)
            conv_half(2, 0, 1)
            dve.wait_ge(in_b, 16)
            dve.wait_ge(y_free, START_Y + 7)
            add_bias(0)
            max_x(3)
            scale_x(3, 1)
            scale_ctx(3)
            dve.wait_ge(l_free, 8)
            leave_first(7)
            split_x(3, 1)
            dve.wait_ge(y_free, START_Y + 8)
            add_bias(1)

            def tile(t, b, conv, split):
                dve.wait_ge(l_free, 4 * t)
                nc.vector.tensor_scalar(yinv[:, b, 0:4], wsc[:, :, 1], sc[:, b, 4:5], None, ALU.mult)
                softmax(t, b)
                if conv:
                    conv_half(t + 1, 1 - b, 0)
                if split:
                    max_x(t + 2)
                dve.wait_ge(xr_in[b], 8 * (t - b) + 16)
                add_bias(b)
                dve.wait_ge(biased, t + 1)
                leave(t, b, 0, Y[0], 4 * t + 1)
                if conv:
                    conv_half(t + 1, 1 - b, 1)
                leave(t, b, 1, Y[1], 4 * t + 2)
                dve.wait_ge(y_free, 4 * t + 1 + START_Y)
                add_lora(t, b, 0, L_BANK[0])
                if split:
                    scale_x(t + 2, b)
                    scale_ctx(t + 2)
                    split_x(t + 2, b)
                leave(t, b, 2, Y[2], 4 * t + 3)
                dve.wait_ge(y_free, 4 * t + 3 + START_Y)
                for oc in range(1, NOC):
                    add_lora(t, b, oc, L_BANK[oc])
                dve.wait_ge(l_free, 4 * t + 4)
                leave(t, b, 3, Y[3], 4 * t + 4)

            with dve.Fori(2, N - 2, 2) as t:
                for b in range(2):
                    tile(t + b, b, True, True)
            tile(N - 2, 0, True, False)
            tile(N - 1, 1, False, False)

        @block.tensor
        def _(pe):
            def conv(n, mb, free):
                pe.wait_ge(bank_free, free)
                for g in range(G):
                    o = C[mb % 2][:, g * P:(g + 1) * P]
                    for a in range(3):
                        for xp, wp in ((0, 0), (0, 1), (1, 0)):
                            mm = nc.tensor.matmul(o, xh[:, xp, g, mb * P + 2 - a:mb * P + 2 - a + P],
                                                  T16[:, wp, g, a * P:(a + 1) * P],
                                                  start=(a == 0 and xp == 0 and wp == 0), stop=(a == 2 and xp == 1))
                mm.then_inc(conv_done, 1)

            def z_products(b, kb, zbank):
                zb = zbank[:, 0:2 * ZC]
                nc.tensor.matmul(zb, h16[:, b, 0, kb, :], A16[:, kb, :], start=kb == 0, stop=False)
                return nc.tensor.matmul(zb[:, 0:ZC], h16[:, b, 1, kb, :], A16[:, kb, 0:ZC], start=False, stop=kb == KB - 1)

            def products(b, oc, bank, fresh=False, zbank=None):
                for kb in range(KB):
                    if fresh:
                        pe.wait_ge(w_lo, oc * KB + kb + 1)
                    hh, hl = h16[:, b, 0, kb, :], h16[:, b, 1, kb, :]
                    nc.tensor.matmul(bank[:, :], hh, wslot(oc, kb, 0), start=kb == 0, stop=False)
                    nc.tensor.matmul(bank[:, :], hh, wslot(oc, kb, 1), start=False, stop=False)
                    my = nc.tensor.matmul(bank[:, :], hl, wslot(oc, kb, 0), start=False, stop=kb == KB - 1)
                    if zbank is not None:
                        mm = z_products(b, kb, zbank)
                my.then_inc(y_done, 1)
                if zbank is not None:
                    mm.then_inc(z_done, 1)

            def turn(b, ready):
                pe.wait_ge(z_ready, ready)
                nc.tensor.transpose(Q[:, b * P:(b + 1) * P], zcat[:, b, :], ident[:, :]).then_inc(z_turned, 1)

            def lora(b, oc, bank):
                nc.tensor.matmul(bank[:, :], zT[0:3 * ZR, b, :], B16[:, oc * OC:(oc + 1) * OC], start=True, stop=True).then_inc(l_done, 1)

            pe.wait_ge(in_ctx, 32)
            pe.wait_ge(padded, 1)
            nc.tensor.matmul(Z[0:N, 0:P], cT_sb, cwT_sb, start=True, stop=False)
            nc.tensor.matmul(Z[0:N, 0:P], onesr[:, 0:N], biasr[:, :], start=False, stop=True).then_inc(ctx_made, 1)
            pe.wait_ge(sel_ready, 1)
            pe.wait_ge(in_A, 16)

            def picked(kb):
                return Y[1 + kb // 8][:, (kb % 8) * ZC:(kb % 8 + 1) * ZC]

            def pick_a(kbs):
                for kb in kbs:
                    mm = nc.tensor.matmul(picked(kb)[:, 0:ZR], A_raw[:, kb * P:(kb + 1) * P], sel[:, 0:ZR], start=True, stop=True)
                mm.then_inc(a_picked, 1)

            pick_a(range(3 * KB // 4))
            pe.wait_ge(padded, 3)
            pe.wait_ge(t_lo, 1)
            pe.wait_ge(x_lo, 1)
            for mb in range(MB):
                conv(0, mb, mb + 1)
            pick_a(range(3 * KB // 4, KB))
            pe.wait_ge(in_R, 16)
            for kb in range(KB):
                mm = nc.tensor.matmul(picked(kb)[:, ZR:ZC], R_raw[:, kb * P:(kb + 1) * P], selr[0:E, :], start=True, stop=True)
            mm.then_inc(a_picked, 1)
            pe.wait_ge(rpb_ready, 1)
            pe.wait_ge(ctx_left, 1)
            nc.tensor.matmul(Z[:, 0:EA], rpbc, selr[0:E, :], start=True, stop=True).then_inc(bias4_made, 1)

            def first(i, fresh=False):
                t, oc = FIRST[i]
                if i >= NOC:
                    pe.wait_ge(y_free, i + 1)
                products(t, oc, Y[i % NOC], fresh=fresh, zbank=Z1 if i == 1 else None)

            pe.wait_ge(h_lo, 4)
            first(0, fresh=True)
            pe.wait_ge(in_B, 16)
            pe.wait_ge(a_left, 2)
            for oc in range(NOC):
                nc.tensor.matmul(B_BANK[oc][0:3 * ZR, :], sel[:, :], B_raw[:, oc * OC:(oc + 1) * OC],
                                 start=True, stop=True).then_inc(b_picked, 1)
            pe.wait_ge(x_lo, 2)
            for mb in range(MB):
                conv(1, mb, MB + mb + 1)
            pe.wait_ge(a_lo, 2)
            pe.wait_ge(bias4_left, 1)
            for kb in range(KB):
                mm = z_products(0, kb, Z)
            mm.then_inc(z_done, 1)
            pe.wait_ge(h_lo, 8)
            pe.wait_ge(b_lo, 2)
            first(1)
            pe.wait_ge(b_lo, NOC)
            first(2, fresh=True)
            first(3)
            turn(0, 2)
            turn(1, 2)
            first(4, fresh=True)
            pe.wait_ge(zT_ready, 2)

            def lora_first(k):
                if k >= 3:
                    pe.wait_ge(l_free, k - 2)
                lora(k // NOC, k % NOC, L_FIRST[k])

            for k in (0, 1, 2):
                lora_first(k)
            first(5)
            for k in (3, 4, 5):
                lora_first(k)
            first(6, fresh=True)
            pe.wait_ge(y_free, START_Y + 6)
            for k in (6, 7):
                lora_first(k)
            pe.wait_ge(x_lo, 3)
            pe.wait_ge(l_free, 5)
            for mb in range(MB):
                conv(2, mb, 2 * MB + mb + 1)
            first(7)

            def tile(t, b, more):
                def chunk(oc):
                    pe.wait_ge(y_free, 4 * t + oc + 1)
                    products(b, oc, Y[oc], zbank=Z if oc == 0 else None)

                pe.wait_ge(h_lo, 4 * (t + 1))
                pe.wait_ge(l_free, 4 * t)
                chunk(0)
                if more:
                    pe.wait_ge(x_lo, t + 2)
                    conv(t + 1, 0, 4 * (t + 1) + 1)
                    conv(t + 1, 1, 4 * (t + 1) + 2)
                chunk(1)
                turn(b, t + 1)
                if more:
                    conv(t + 1, 2, 4 * (t + 1) + 3)
                    conv(t + 1, 3, 4 * (t + 1) + 4)
                pe.wait_ge(zT_ready, t + 1)
                if more:
                    pe.wait_ge(bank_free, START_C + 4 * (t + 1) + 3)
                lora(b, 0, L_BANK[0])
                chunk(2)
                if more:
                    pe.wait_ge(bank_free, START_C + 4 * (t + 1) + 4)
                lora(b, 1, L_BANK[1])
                pe.wait_ge(l_free, 4 * t + 1)
                lora(b, 2, L_BANK[2])
                lora(b, 3, L_BANK[3])
                chunk(3)

            with pe.Fori(2, N - 2, 2) as t:
                for b in range(2):
                    tile(t + b, b, True)
            tile(N - 2, 0, True)
            tile(N - 1, 1, False)


_OUT = (N, P, L)


def kernel(**inputs):
    import numpy as np
    import concourse.bacc as bacc
    from concourse.bass_utils import run_bass_kernel_spmd as run

    i = {k: np.asarray(v) for k, v in inputs.items()}
    arrays = {
        "xc": i["x"].reshape(N, G, CG, M, R).transpose(0, 4, 2, 1, 3).reshape(N, P, G, M),
        "xr": i["x"],
        "wconv": i["L0_cond_weight"].reshape(G, CG, CG, K)[:, :, :, ::-1].transpose(2, 0, 3, 1).reshape(CG, G, K * CG),
        "ctx_w": np.concatenate([i["cond_128"].T, i["L0_cond_c_weight"].T], 1),
        "bias": i["fside_S_0"].reshape(1, P),
        "cw": i["L0_cond_weight"].reshape(P, CG * K),
        "wt": i["L0_ffn_W_base"].reshape(NOC, OC, MB, P, R).transpose(0, 3, 2, 4, 1).reshape(NOC, P, KB * OC),
        "loraA": i["L0_ffn_lora_A"].reshape(E * RK, MB, P, R).transpose(0, 1, 3, 2).reshape(E * RK, L),
        "routerW": i["L0_ffn_router_W"].reshape(E, MB, P, R).transpose(0, 1, 3, 2).reshape(E, L),
        "loraB": i["L0_ffn_lora_B"].transpose(0, 2, 1).reshape(E * RK, O),
        "b_base": i["L0_ffn_b_base"].reshape(1, O),
        "router_bp": np.stack([i["L0_ffn_router_b"], i["L0_ffn_domain_prior"]], 1),
        "active": i["L0_ffn_active"].reshape(1, EA),
    }
    arrays = {k: np.ascontiguousarray(v) for k, v in arrays.items()}
    nc = bacc.Bacc("TRN2", target_bir_lowering=False, num_devices=1, dynamic_dma_scratch_size=4096)
    args = [nc.dram_tensor(k, v.shape, mybir.dt.from_np(v.dtype), kind="ExternalInput").ap() for k, v in arrays.items()]
    args.append(nc.dram_tensor("out", _OUT, F32, kind="ExternalOutput").ap())
    adaln_ffn(nc, *args)
    return run(nc, [arrays], core_ids=[0]).results[0]["out"]
```
